# Optimizing a Trainium2 kernel written in Bass

```python
import numpy as np
import jax
import jax.numpy as jnp

def _softmax(x, axis=-1):
    return jax.nn.softmax(x, axis=axis)

def _gelu(x):
    return jax.nn.gelu(x, approximate=True)

def _silu(x):
    return jax.nn.silu(x)

def _sigmoid(x):
    return jax.nn.sigmoid(x)

def _layernorm(x, axis=-1, eps=1e-05):
    m = jnp.mean(x, axis=axis, keepdims=True)
    v = jnp.var(x, axis=axis, keepdims=True)
    return (x - m) / jnp.sqrt(v + eps)

def _scatter_add(tgt, idx, src, axis=0):
    return tgt.at[idx].add(src)

def _segment_sum(src, seg, n):
    return jax.ops.segment_sum(src, seg, n)
kernel_name = 'mk_adaln_ffn_d1_seqx_r8_c1958a'

def setup_inputs(seed: int=0):
    np.random.seed(seed)
    _w = jnp.asarray

    def _rec_inputs():
        import jax
        import jax.numpy as jnp
        _rk = jax.random.key(seed)
        x = -0.000125 + 0.9999 * jax.random.normal(jax.random.fold_in(_rk, 1), (32, 32, 128), jnp.float32)
        _lenS = 32 - jax.random.randint(jax.random.fold_in(_rk, 7), (32,), 0, max(1, 32 // 4) + 1, jnp.int32)
        _lenS2 = 32 - jax.random.randint(jax.random.fold_in(_rk, 8), (32,), 0, max(1, 32 // 4) + 1, jnp.int32)
        cond_1024 = -0.00493535 + 1.00056 * jax.random.normal(jax.random.fold_in(_rk, 11), (32, 128), jnp.float32)
        return (x, cond_1024)
    x, cond_1024 = _rec_inputs()

    def _L0_cond_setup():
        import jax, jax.numpy as jnp
        import numpy as np
        N, T, D, H = (64, 64, 128, 128)
        key = jax.random.key(seed)
        k1, k2, k3, k4 = jax.random.split(key, 4)
        x = jax.random.normal(k1, (N, T, D), dtype=jnp.float32)
        h0 = jax.random.normal(k2, (N, H), dtype=jnp.float32)
        Wx = jax.random.normal(k3, (D, H), dtype=jnp.float32) / jnp.sqrt(jnp.float32(D))
        Wh = jax.random.normal(k4, (H, H), dtype=jnp.float32) / jnp.sqrt(jnp.float32(H))
        b = jnp.zeros((H,), dtype=jnp.float32)
        return {'x': x, 'h0': h0, 'Wx': Wx, 'Wh': Wh, 'b': b}
    _L0_cond_all = _L0_cond_setup()
    _L0_cond_in = {k: v for k, v in _L0_cond_all.items() if k in ('Wx', 'Wh', 'b')}
    del _L0_cond_all

    def _L0_ffn_setup():
        import jax, jax.numpy as jnp
        import numpy as np
        H = 128
        I = 128
        E = 16
        K = 4
        LIMIT = 7.0
        ALPHA = 1.702
        EPS = 1e-05
        key = jax.random.key(seed)
        ks = jax.random.split(key, 8)
        x = jax.random.normal(ks[0], (2, 64, H), dtype=jnp.float32)
        norm_scale = jnp.ones((H,), dtype=jnp.float32)
        wg = jax.random.normal(ks[1], (H, E), dtype=jnp.float32) * 0.02
        bg = jax.random.normal(ks[2], (E,), dtype=jnp.float32) * 0.02
        w1 = jax.random.normal(ks[3], (E, H, 2 * I), dtype=jnp.float32) * 0.02
        b1 = jax.random.normal(ks[4], (E, 2 * I), dtype=jnp.float32) * 0.02
        w2 = jax.random.normal(ks[5], (E, I, H), dtype=jnp.float32) * 0.02
        b2 = jax.random.normal(ks[6], (E, H), dtype=jnp.float32) * 0.02
        return {'x': x, 'norm_scale': norm_scale, 'wg': wg, 'bg': bg, 'w1': w1, 'b1': b1, 'w2': w2, 'b2': b2}
    _L0_ffn_all = _L0_ffn_setup()
    _L0_ffn_in = {k: v for k, v in _L0_ffn_all.items() if k in ('norm_scale', 'wg', 'bg', 'w1', 'b1', 'w2', 'b2')}
    del _L0_ffn_all
    return {'x': x, 'cond_1024': cond_1024, 'L0_cond_Wx': _L0_cond_in['Wx'], 'L0_cond_Wh': _L0_cond_in['Wh'], 'L0_cond_b': _L0_cond_in['b'], 'L0_ffn_norm_scale': _L0_ffn_in['norm_scale'], 'L0_ffn_wg': _L0_ffn_in['wg'], 'L0_ffn_bg': _L0_ffn_in['bg'], 'L0_ffn_w1': _L0_ffn_in['w1'], 'L0_ffn_b1': _L0_ffn_in['b1'], 'L0_ffn_w2': _L0_ffn_in['w2'], 'L0_ffn_b2': _L0_ffn_in['b2']}

def reference(x, cond_1024, L0_cond_Wx, L0_cond_Wh, L0_cond_b, L0_ffn_norm_scale, L0_ffn_wg, L0_ffn_bg, L0_ffn_w1, L0_ffn_b1, L0_ffn_w2, L0_ffn_b2):
    import jax
    import jax.numpy as jnp

    def _L0_cond_ref(x, h0, Wx, Wh, b):
        import jax, jax.numpy as jnp
        import numpy as np
        N, T, D, H = (64, 64, 128, 128)
        xw = jnp.einsum('ntd,dh->nth', x, Wx) + b

        def step(prev_h, xw_t):
            next_h = jnp.tanh(xw_t + prev_h @ Wh)
            return (next_h, next_h)
        _, hs = jax.lax.scan(step, h0, jnp.swapaxes(xw, 0, 1))
        return jnp.swapaxes(hs, 0, 1)

    def _L0_ffn_ref(x, norm_scale, wg, bg, w1, b1, w2, b2):
        import jax, jax.numpy as jnp
        import numpy as np
        H = 128
        I = 128
        E = 16
        K = 4
        LIMIT = 7.0
        ALPHA = 1.702
        EPS = 1e-05
        shape = x.shape
        xf = x.reshape(-1, shape[-1])
        xn = xf * jax.lax.rsqrt(jnp.mean(xf * xf, axis=-1, keepdims=True) + EPS) * norm_scale
        logits = xn @ wg + bg
        vals, idx = jax.lax.top_k(logits, K)
        gates = jax.nn.softmax(vals, axis=-1)
        gate_full = jnp.einsum('tke,tk->te', jax.nn.one_hot(idx, E, dtype=gates.dtype), gates)
        h = jnp.einsum('th,ehd->etd', xn, w1) + b1[:, None, :]
        a = jnp.minimum(h[..., ::2], LIMIT)
        b = jnp.clip(h[..., 1::2], -LIMIT, LIMIT)
        s = a * jax.nn.sigmoid(ALPHA * a) * (b + 1.0)
        y = jnp.einsum('eti,eih->eth', s, w2) + b2[:, None, :]
        t = jnp.einsum('eth,te->th', y, gate_full)
        return x + t.reshape(shape)
    x = x + _L0_ffn_ref(_L0_cond_ref(x, cond_1024, L0_cond_Wx, L0_cond_Wh, L0_cond_b), L0_ffn_norm_scale, L0_ffn_wg, L0_ffn_bg, L0_ffn_w1, L0_ffn_b1, L0_ffn_w2, L0_ffn_b2)
    return x

_drawn_inputs = setup_inputs


def setup_inputs(seed=0):
    import zlib

    import numpy as np

    out = dict(_drawn_inputs(seed))
    spreads = {'L0_cond_b': (0.0, 0.1), 'L0_ffn_norm_scale': (1.0, 0.6)}
    factors = {'L0_ffn_wg': 4.586,
     'L0_ffn_bg': 8.0,
     'L0_ffn_w1': 4.882,
     'L0_ffn_b1': 8.0,
     'L0_ffn_w2': 4.819,
     'L0_ffn_b2': 6.78}
    for name, (base, spread) in spreads.items():
        noise = np.random.default_rng([zlib.crc32(name.encode()), seed]).standard_normal(out[name].shape)
        drawn = base * np.exp(spread * noise) if base else spread * noise
        out[name] = jnp.asarray(drawn.astype(out[name].dtype))
    for name, factor in factors.items():
        out[name] = (out[name] * factor).astype(out[name].dtype)
    return out
```

```python
import concourse.bass as bass
from concourse import mybir
from contextlib import ExitStack



def adaln_rnn_moe_kernel(nc, x, cond, wx, wh, b, norm_scale, wg, bg, w1, b1, w2, b2, out):
    F32 = mybir.dt.float32
    F32R = mybir.dt.float32r
    U32 = mybir.dt.uint32
    ALU = mybir.AluOpType
    ACT = mybir.ActivationFunctionType
    AX = mybir.AxisListType

    N, T, D = x.shape
    E, H, I2 = w1.shape
    P = 128
    K = 4
    LIMIT, EPS = 7.0, 1e-05
    TL = P // N
    NT = N * T // P
    NCH = 2
    TC = NT // NCH
    CW = TC * P
    SC = T // NCH
    NI = NCH * E
    NG = 4
    EG = E // NG
    LAG = 3
    GR = 3 * E

    ctx = ExitStack()
    with ctx:
        def sb(name, shape, dt=F32):
            return ctx.enter_context(nc.sbuf_tensor(name, shape, dt))

        def pb(name):
            return ctx.enter_context(nc.psum_tensor(name, [P, 512], F32))

        def sem(name):
            return ctx.enter_context(nc.semaphore(name))

        rows = sb("rows", [N + 2, D])
        wx_sb = sb("wx_sb", [D, H])
        wh_sb = sb("wh_sb", [H, H])
        x_sb = sb("x_sb", [P, NT, D])
        b1_sb = sb("b1_sb", [E, I2])
        wg_sb = sb("wg_sb", [H, E])
        bg_sb = sb("bg_sb", [P, E])
        b2_sb = sb("b2_sb", [GR, H])
        w1_sb = sb("w1_sb", [H, E, I2])
        w2_sb = sb("w2_sb", [P, E, H])
        ident = sb("ident", [P, P])
        zero_one = sb("zero_one", [P, P])
        ones = sb("ones", [P, 1])
        neg_half = sb("neg_half", [P, 1])
        euler = sb("euler", [P, TC * K])
        limit_col = sb("limit_col", [P, 1])
        iota_e = sb("iota_e", [P, E])
        pair_id = sb("pair_id", [P, E])
        select = sb("select", [P, E, P], F32R)
        wg_scaled = sb("wg_scaled", [H, E])
        b_col = sb("b_col", [P, 2])
        lim_b1a = sb("lim_b1a", [P, E])
        one_b1b = sb("one_b1b", [P, E])
        b2_hi = sb("b2_hi", [GR, H], F32R)
        b2_rows = sb("b2_rows", [P, H], F32R)
        w1_hi = sb("w1_hi", [H, E, 2, P], F32R)
        w1_lo = sb("w1_lo", [H, E, 2, P], F32R)
        w2_hi = sb("w2_hi", [P, E, H], F32R)
        w2_lo = sb("w2_lo", [P, E, H], F32R)
        xT = sb("xT", [D, NT * P])
        hT = sb("hT", [H, (T + 1) * N])
        sq = sb("sq", [H, NT * P])
        xn = sb("xn", [H, NT * P])
        xn_hi = sb("xn_hi", [H, NT * P], F32R)
        xn_lo = sb("xn_lo", [H, NT * P], F32R)
        meansq = sb("meansq", [P, NT])
        rstd = sb("rstd", [P, NT])
        raw = sb("raw", [P, NT, E])
        logits = sb("logits", [P, NT, E])
        top = sb("top", [P, NT, 8])
        top_i = sb("top_i", [P, NT, 8], U32)
        top_f = sb("top_f", [P, NT, K])
        diff = sb("diff", [P, NT, K])
        expo = sb("expo", [P, NT, K])
        den = sb("den", [P, NT])
        inv = sb("inv", [P, NT])
        gate_k = sb("gate_k", [P, NT, K])
        hot = sb("hot", [P, NT, E, K])
        hot_g = sb("hot_g", [P, NT, E, K])
        gates = sb("gates", [P, NT, E])
        gate_parts = sb("gate_parts", [P, NT, GR], F32R)
        gT = sb("gT", [P, NT * P], F32R)
        relu_a = sb("relu_a", [P, 2, CW])
        swish = sb("swish", [P, 2, CW])
        lin = sb("lin", [P, 2, CW])
        act = sb("act", [P, 2, CW])
        actg = sb("actg", [P, 2, CW])
        act_hi = sb("act_hi", [P, 4, CW], F32R)
        act_lo = sb("act_lo", [P, 4, CW], F32R)
        yT = sb("yT", [P, NCH, CW])
        y_sb = sb("y_sb", [P, NT, D])

        psA = [pb("psA0"), pb("psA1")]
        psB = [pb("psB0"), pb("psB1")]
        psG, psY, psR, psM = pb("psG"), pb("psY"), pb("psR"), pb("psM")

        rows_loaded = sem("rows_loaded")
        rnn_w_loaded = sem("rnn_w_loaded")
        x_loaded = [sem(f"x_loaded{c}") for c in range(NCH)]
        b1_loaded = sem("b1_loaded")
        wg_loaded = sem("wg_loaded")
        bg_loaded = sem("bg_loaded")
        b2_loaded = sem("b2_loaded")
        w1_loaded = [sem(f"w1_loaded{g}") for g in range(NG)]
        w2_loaded = [sem(f"w2_loaded{g}") for g in range(NG)]
        consts_ready = sem("consts_ready")
        rows_t = sem("rows_t")
        rows_read = sem("rows_read")
        b1_t = sem("b1_t")
        b1_read = sem("b1_read")
        x_t = sem("x_t")
        xT_ready = sem("xT_ready")
        wg_ready = sem("wg_ready")
        b2_ready = sem("b2_ready")
        gT_zeroed = sem("gT_zeroed")
        select_ready = sem("select_ready")
        w1_ready = sem("w1_ready")
        w2_ready = sem("w2_ready")
        step_mm = sem("step_mm")
        step_done = sem("step_done")
        sq_ready = sem("sq_ready")
        stats_mm = sem("stats_mm")
        stats_read = sem("stats_read")
        rstd_ready = sem("rstd_ready")
        rstd_mm = sem("rstd_mm")
        rstd_read = sem("rstd_read")
        xn_ready = sem("xn_ready")
        diff_ready = sem("diff_ready")
        expo_ready = sem("expo_ready")
        parts_ready = sem("parts_ready")
        gT_mm = sem("gT_mm")
        gT_ready = sem("gT_ready")
        a_mm = sem("a_mm")
        b_mm = sem("b_mm")
        g_mm = sem("g_mm")
        y_mm = sem("y_mm")
        relu_done = sem("relu_done")
        swish_done = sem("swish_done")
        lin_done = sem("lin_done")
        act_done = sem("act_done")
        actg_done = sem("actg_done")
        hi_done = sem("hi_done")
        lo_done = sem("lo_done")
        yT_ready = sem("yT_ready")
        y_t = sem("y_t")
        y_ready = sem("y_ready")
        stored = sem("stored")
        dve_chain = sem("dve_chain")
        pool_chain = sem("pool_chain")

        block = ctx.enter_context(nc.Block())

        x_v = x.rearrange("n (j s) d -> s n j d", s=TL)
        out_v = out.rearrange("n (j s) d -> s n j d", s=TL)
        w1_v = w1.rearrange("e h i -> h e i")
        w2_v = w2.rearrange("e i h -> i e h")

        def tok(j, n=1):
            return slice(j * P, (j + n) * P)

        def htok(j):
            return slice(N + j * P, N + (j + 1) * P)

        def chunk(c):
            return slice(c * CW, (c + 1) * CW)

        def step_psum(t):
            if t < TL:
                return psA[0][:, t * N:(t + 1) * N]
            if t < SC:
                return psA[1][:, (t - TL) * N:(t - TL + 1) * N]
            return psR[:, (t - SC) * N:(t - SC + 1) * N]

        def pre_psum(j):
            bank, at = (psA[0], 0) if j == 0 else (psA[1], j - 1) if j < TC else (psR, j - TC)
            return bank[:, at * P:(at + 1) * P], at == 0

        STEPS_PER_IT = 2

        def square_it(j):
            return (TL * (j + 1) - 1 - SC) // STEPS_PER_IT + 1

        LATE = range(TC, NT)
        GATE_IT = square_it(NT - 1) + 3
        OUT_IT = E + LAG + 2

        @block.sync
        def _(sp):
            sp.dma_start(rows[0:N, :], cond).then_inc(rows_loaded, 16)
            sp.dma_start(rows[N:N + 1, :], b.rearrange("(a n) -> a n", a=1)).then_inc(rows_loaded, 16)
            sp.dma_start(rows[N + 1:N + 2, :], norm_scale.rearrange("(a n) -> a n", a=1)).then_inc(rows_loaded, 16)
            sp.dma_start(wx_sb[:, :], wx).then_inc(rnn_w_loaded, 16)
            sp.dma_start(wh_sb[:, :], wh).then_inc(rnn_w_loaded, 16)
            for g in range(NG):
                ge = slice(g * EG, (g + 1) * EG)
                sp.dma_start(w1_sb[:, ge, :], w1_v[:, ge, :]).then_inc(w1_loaded[g], 16)
                sp.dma_start(w2_sb[:, ge, :], w2_v[:, ge, :]).then_inc(w2_loaded[g], 16)
            for c in range(NCH):
                sp.wait_ge(y_ready, c + 1)
                cj = slice(c * TC, (c + 1) * TC)
                for s in range(TL):
                    sp.dma_start(out_v[s][:, cj, :], y_sb[s * N:(s + 1) * N, cj, :]).then_inc(stored, 16)
            sp.wait_ge(stored, 16 * TL * NCH)

        @block.gpsimd
        def _(pool):
            chain = [0]

            def link(ins):
                chain[0] += 1
                ins.then_inc(pool_chain, 1)
                pool.wait_ge(pool_chain, chain[0])

            link(nc.gpsimd.memset(zero_one[:, :], 0.0))
            nc.gpsimd.affine_select(out=ident[:, :], in_=zero_one[:, :], compare_op=ALU.not_equal, fill=1.0, base=0,
                                    pattern=[[-1, P]], channel_multiplier=1).then_inc(consts_ready, 1)
            pool.dma_start(b1_sb[:, :], b1).then_inc(b1_loaded, 16)
            pool.dma_start(wg_sb[:, :], wg).then_inc(wg_loaded, 16)
            pool.dma_start(bg_sb[:, :], bg.partition_broadcast(P)).then_inc(bg_loaded, 16)
            for r in range(3):
                pool.dma_start(b2_sb[r * E:(r + 1) * E, :], b2).then_inc(b2_loaded, 16)
            nc.gpsimd.memset(ones[:, :], 1.0)
            nc.gpsimd.memset(neg_half[:, :], -0.5)
            nc.gpsimd.memset(euler[:, :], 2.718281828459045)
            nc.gpsimd.memset(limit_col[:, :], LIMIT)
            nc.gpsimd.iota(iota_e[:, :], pattern=[[1, E]], base=0, channel_multiplier=0,
                           allow_small_or_imprecise_dtypes=True).then_inc(consts_ready, 1)

            def power_rstd(j):
                pool.wait_ge(stats_read, j + 1)
                nc.gpsimd.tensor_tensor(rstd[:, j:j + 1], meansq[:, j:j + 1], neg_half[:, :],
                                        ALU.pow).then_inc(rstd_ready, 1)

            def power_expo(c):
                pool.wait_ge(diff_ready, c + 1)
                d = diff[:, c * TC:(c + 1) * TC, :].rearrange("p j k -> p (j k)")
                o = expo[:, c * TC:(c + 1) * TC, :].rearrange("p j k -> p (j k)")
                nc.gpsimd.tensor_tensor(o, euler[:, :], d, ALU.pow).then_inc(expo_ready, 1)

            def split_w2(g):
                ge = slice(g * EG, (g + 1) * EG)
                pool.wait_ge(w2_loaded[g], 16)
                link(nc.gpsimd.tensor_copy(w2_hi[:, ge, :], w2_sb[:, ge, :]))
                nc.gpsimd.tensor_tensor(w2_lo[:, ge, :], w2_sb[:, ge, :], w2_hi[:, ge, :].bitcast(F32),
                                        ALU.subtract).then_inc(w2_ready, 1)

            for j in range(TC):
                power_rstd(j)
                if j < TC - 1:
                    split_w2(j)
            power_expo(0)
            split_w2(NG - 1)
            for i in range(NI + 1):
                if i >= 1:
                    q = i - 1
                    pool.wait_ge(hi_done, q + 1)
                    if q >= 4:
                        pool.wait_ge(y_mm, q - 3)
                    nc.gpsimd.tensor_tensor(act_lo[:, q % 4, :], actg[:, q % 2, :],
                                            act_hi[:, q % 4, :].bitcast(F32),
                                            ALU.subtract).then_inc(lo_done, 1)
                for j in LATE:
                    if i == square_it(j) + 1:
                        power_rstd(j)
                if i == GATE_IT:
                    power_expo(1)

        @block.scalar
        def _(acte):
            for c in range(NCH):
                cj = slice(c * TC, (c + 1) * TC)
                for s in range(TL):
                    acte.dma_start(x_sb[s * N:(s + 1) * N, cj, :], x_v[s][:, cj, :]).then_inc(x_loaded[c], 16)

            def tanh(t):
                if t == 0:
                    acte.wait_ge(rows_read, 1)
                acte.wait_ge(step_mm, t + 1)
                nc.scalar.activation(hT[:, (t + 1) * N:(t + 2) * N], step_psum(t), ACT.Tanh,
                                     bias=b_col[:, 0:1]).then_inc(step_done, 1)

            for t in range(SC):
                tanh(t)
            acte.wait_ge(b1_read, 1)
            acte.wait_ge(consts_ready, 2)
            for i in range(NI + 2):
                if i < NI:
                    e = i % E
                    acte.wait_ge(a_mm, i + 1)
                    if i >= 2:
                        acte.wait_ge(swish_done, i - 1)
                    nc.scalar.activation(relu_a[:, i % 2, :], psA[i % 2][:, 0:CW], ACT.Relu, scale=-1.0,
                                         bias=lim_b1a[:, e:e + 1]).then_inc(relu_done, 1)
                if SC + STEPS_PER_IT * i < T:
                    tanh(SC + STEPS_PER_IT * i)
                if i < NI:
                    acte.wait_ge(relu_done, i + 1)
                    if i >= 2:
                        acte.wait_ge(act_done, i - 1)
                    nc.scalar.activation(swish[:, i % 2, :], relu_a[:, i % 2, :], ACT.Gelu_apprx_sigmoid,
                                         scale=-1.0, bias=limit_col[:, :]).then_inc(swish_done, 1)
                if SC + STEPS_PER_IT * i + 1 < T:
                    tanh(SC + STEPS_PER_IT * i + 1)
                if 1 <= i <= NI:
                    q = i - 1
                    acte.wait_ge(actg_done, q + 1)
                    if q >= 4:
                        acte.wait_ge(y_mm, q - 3)
                    nc.scalar.activation(act_hi[:, q % 4, :], actg[:, q % 2, :], ACT.Copy).then_inc(hi_done, 1)

        @block.vector
        def _(dve):
            chain = [0]

            def link(ins):
                chain[0] += 1
                ins.then_inc(dve_chain, 1)
                dve.wait_ge(dve_chain, chain[0])

            def square(j):
                dve.wait_ge(step_done, TL * (j + 1))
                nc.vector.tensor_tensor(sq[:, tok(j)], hT[:, htok(j)], hT[:, htok(j)], ALU.mult).then_inc(sq_ready, 1)

            def stats(j):
                dve.wait_ge(stats_mm, j + 1)
                nc.vector.tensor_copy(raw[:, j, :], psM[:, 16:16 + E])
                nc.vector.tensor_scalar(meansq[:, j:j + 1], psM[:, 0:1], 1.0 / H, EPS, ALU.mult,
                                        ALU.add).then_inc(stats_read, 1)

            def normalise(j):
                dve.wait_ge(rstd_mm, j + 1)
                nc.vector.scalar_tensor_tensor(xn[:, tok(j)], hT[:, htok(j)], b_col[:, 1:2], psM[:, P:2 * P],
                                               ALU.mult, ALU.mult).then_inc(rstd_read, 1)
                dve.wait_ge(rstd_read, j + 1)
                link(nc.vector.tensor_copy(xn_hi[:, tok(j)], xn[:, tok(j)]))
                nc.vector.tensor_tensor(xn_lo[:, tok(j)], xn[:, tok(j)], xn_hi[:, tok(j)].bitcast(F32),
                                        ALU.subtract).then_inc(xn_ready, 1)

            def route(j):
                if j == 0:
                    dve.wait_ge(bg_loaded, 16)
                link(nc.vector.scalar_tensor_tensor(logits[:, j, :], raw[:, j, :], rstd[:, j:j + 1], bg_sb[:, :],
                                                    ALU.mult, ALU.add))
                link(nc.vector.max(top[:, j, :], logits[:, j, :]))
                link(nc.vector.max_index(top_i[:, j, :], top[:, j, :], logits[:, j, :]))

            def gates_start(c):
                cj = slice(c * TC, (c + 1) * TC)
                nc.vector.tensor_tensor(diff[:, cj, :], top[:, cj, 0:K], top[:, cj, 0:1].to_broadcast([P, TC, K]),
                                        ALU.subtract).then_inc(diff_ready, 1)
                link(nc.vector.tensor_copy(top_f[:, cj, :], top_i[:, cj, 0:K]))
                for j in range(c * TC, (c + 1) * TC):
                    last = nc.vector.tensor_tensor(
                        hot[:, j, :, :], iota_e[:, :].rearrange("p (e o) -> p e o", o=1).to_broadcast([P, E, K]),
                        top_f[:, j:j + 1, :].to_broadcast([P, E, K]), ALU.is_equal)
                link(last)

            def gates_finish(c):
                cj = slice(c * TC, (c + 1) * TC)
                dve.wait_ge(expo_ready, c + 1)
                link(nc.vector.tensor_reduce(den[:, cj], expo[:, cj, :], AX.X, ALU.add))
                link(nc.vector.reciprocal(inv[:, cj], den[:, cj]))
                link(nc.vector.tensor_tensor(
                    gate_k[:, cj, :], expo[:, cj, :],
                    inv[:, cj].rearrange("p (j o) -> p j o", o=1).to_broadcast([P, TC, K]), ALU.mult))
                for j in range(c * TC, (c + 1) * TC):
                    last = nc.vector.tensor_tensor(hot_g[:, j, :, :], hot[:, j, :, :],
                                                   gate_k[:, j:j + 1, :].to_broadcast([P, E, K]), ALU.mult)
                link(last)
                link(nc.vector.tensor_reduce(gates[:, cj, :], hot_g[:, cj, :, :], AX.X, ALU.add))
                link(nc.vector.tensor_copy(gate_parts[:, cj, 0:E], gates[:, cj, :]))
                nc.vector.tensor_copy(gate_parts[:, cj, 2 * E:3 * E], gates[:, cj, :])
                nc.vector.tensor_tensor(gate_parts[:, cj, E:2 * E], gates[:, cj, :],
                                        gate_parts[:, cj, 0:E].bitcast(F32), ALU.subtract).then_inc(parts_ready, 1)

            def gates_copy(c):
                if c == 0:
                    dve.wait_ge(gT_zeroed, 1)
                dve.wait_ge(gT_mm, c + 1)
                nc.vector.tensor_copy(gT[0:GR, chunk(c)], psM[0:GR, 0:CW]).then_inc(gT_ready, 1)

            def split_w1(g):
                ge = slice(g * EG, (g + 1) * EG)
                src = w1_sb[:, ge, :].rearrange("h e (i a) -> h e a i", a=2)
                dve.wait_ge(w1_loaded[g], 16)
                for a in range(2):
                    last = nc.vector.tensor_copy(w1_hi[:, ge, a, :], src[:, :, a, :])
                link(last)
                for a in range(2):
                    last = nc.vector.tensor_tensor(w1_lo[:, ge, a, :], src[:, :, a, :],
                                                   w1_hi[:, ge, a, :].bitcast(F32), ALU.subtract)
                last.then_inc(w1_ready, 1)

            def add_h(c):
                dve.wait_ge(y_mm, (c + 1) * E)
                nc.vector.tensor_tensor(yT[:, c, :], hT[:, N + c * CW:N + (c + 1) * CW], psY[:, 0:CW],
                                        ALU.add).then_inc(yT_ready, 1)

            def finish_rows(c):
                cj = slice(c * TC, (c + 1) * TC)
                dve.wait_ge(y_t, c + 1)
                nc.vector.tensor_tensor(y_sb[:, cj, :], x_sb[:, cj, :], psM[:, 0:CW].rearrange("p (j d) -> p j d", d=D),
                                        ALU.add).then_inc(y_ready, 1)

            dve.wait_ge(rows_t, 1)
            nc.vector.tensor_copy(hT[:, 0:N], psM[:, 0:N])
            nc.vector.tensor_copy(b_col[:, :], psM[:, N:N + 2]).then_inc(rows_read, 1)
            dve.wait_ge(x_t, 1)
            nc.vector.tensor_copy(xT[:, tok(0)], psB[0][:, 0:P]).then_inc(xT_ready, 1)
            dve.wait_ge(x_t, 2)
            nc.vector.tensor_copy(xT[:, tok(1, TC - 1)], psB[1][:, 0:(TC - 1) * P]).then_inc(xT_ready, 1)
            dve.wait_ge(x_t, 3)
            nc.vector.tensor_copy(xT[:, tok(TC, TC)], psG[:, 0:CW]).then_inc(xT_ready, 1)
            dve.wait_ge(b1_t, 1)
            nc.vector.tensor_scalar(lim_b1a[:, :], psM[:, 64:64 + E], -1.0, LIMIT, ALU.mult, ALU.add)
            nc.vector.tensor_scalar(one_b1b[:, :], psM[:, 80:80 + E], 1.0, None, ALU.add).then_inc(b1_read, 1)
            dve.wait_ge(wg_loaded, 16)
            dve.wait_ge(rows_read, 1)
            nc.vector.tensor_scalar(wg_scaled[:, :], wg_sb[:, :], b_col[:, 1:2], None, ALU.mult).then_inc(wg_ready, 1)
            link(nc.vector.tensor_tensor(pair_id[:, :], ident[:, 0:E], ident[:, E:2 * E], ALU.add))
            nc.vector.tensor_copy(select[:, :, :], pair_id[:, :].rearrange("p (e o) -> p e o", o=1)
                                  .to_broadcast([P, E, P])).then_inc(select_ready, 1)
            link(nc.vector.memset(b2_rows[:, :].bitcast(F32), 0.0))
            nc.vector.memset(gT[:, :].bitcast(F32), 0.0).then_inc(gT_zeroed, 1)
            dve.wait_ge(b2_loaded, 48)
            link(nc.vector.tensor_copy(b2_hi[:, :], b2_sb[:, :]))
            nc.vector.tensor_copy(b2_rows[0:2 * E, :], b2_sb[0:2 * E, :])
            nc.vector.tensor_tensor(b2_rows[2 * E:3 * E, :], b2_sb[2 * E:3 * E, :], b2_hi[2 * E:3 * E, :].bitcast(F32),
                                    ALU.subtract).then_inc(b2_ready, 1)
            dve.wait_ge(consts_ready, 2)
            for j in range(TC):
                split_w1(j)
                square(j)
                stats(j)
                normalise(j)
                route(j)
            gates_start(0)

            for i in range(NI + 1):
                if i < NI:
                    e = i % E
                    dve.wait_ge(b_mm, i + 1)
                    if i >= 2:
                        dve.wait_ge(act_done, i - 1)
                    nc.vector.tensor_scalar(lin[:, i % 2, :], psB[i % 2][:, 0:CW], one_b1b[:, e:e + 1], LIMIT + 1.0,
                                            ALU.add, ALU.min).then_inc(lin_done, 1)
                if i == 0:
                    gates_finish(0)
                    gates_copy(0)
                if i >= 1:
                    q = i - 1
                    dve.wait_ge(g_mm, q + 1)
                    dve.wait_ge(act_done, q + 1)
                    if q >= 2:
                        dve.wait_ge(lo_done, q - 1)
                    nc.vector.tensor_tensor(actg[:, q % 2, :], act[:, q % 2, :], psG[:, 0:CW],
                                            ALU.mult).then_inc(actg_done, 1)
                if i < NI:
                    dve.wait_ge(swish_done, i + 1)
                    dve.wait_ge(lin_done, i + 1)
                    if i >= 2:
                        dve.wait_ge(actg_done, i - 1)
                    nc.vector.scalar_tensor_tensor(act[:, i % 2, :], lin[:, i % 2, :], 1.0 - LIMIT, swish[:, i % 2, :],
                                                   ALU.max, ALU.mult).then_inc(act_done, 1)
                for j in LATE:
                    if i == square_it(j):
                        square(j)
                    if i == square_it(j) + 1:
                        stats(j)
                    if i == square_it(j) + 2:
                        normalise(j)
                        route(j)
                if i == GATE_IT:
                    gates_start(1)
                if i == GATE_IT + 1:
                    gates_finish(1)
                if i == GATE_IT + 2:
                    gates_copy(1)
                if i == OUT_IT - 2:
                    add_h(0)
                if i == OUT_IT:
                    finish_rows(0)
            add_h(1)
            finish_rows(1)

        @block.tensor
        def _(pe):
            def transpose_x(j0, n, bank):
                for j in range(j0, j0 + n):
                    last = nc.tensor.transpose(bank[:, (j - j0) * P:(j - j0 + 1) * P], x_sb[:, j, :], ident[:, :])
                last.then_inc(x_t, 1)

            def pre(j):
                pe.wait_ge(xT_ready, 1 if j == 0 else 2 if j < TC else 3)
                o, first = pre_psum(j)
                nc.tensor.matmul(o, wx_sb[:, :], xT[:, tok(j)], start=first, stop=True, skip_group_check=True)

            def step(t):
                if t:
                    pe.wait_ge(step_done, t)
                nc.tensor.matmul(step_psum(t), wh_sb[:, :], hT[:, t * N:(t + 1) * N], start=False, stop=True,
                                 skip_group_check=True).then_inc(step_mm, 1)

            def stats(j):
                pe.wait_ge(sq_ready, j + 1)
                if j == 0:
                    pe.wait_ge(wg_ready, 1)
                    pe.wait_ge(b1_read, 1)
                else:
                    pe.wait_ge(rstd_read, j)
                if j == TC:
                    pe.wait_ge(gT_ready, 1)
                nc.tensor.matmul(psM[:, 0:1], sq[:, tok(j)], ones[:, :], start=True, stop=True)
                nc.tensor.matmul(psM[:, 16:16 + E], hT[:, htok(j)], wg_scaled[:, :], start=True,
                                 stop=True).then_inc(stats_mm, 1)

            def lay_rstd(j):
                pe.wait_ge(rstd_ready, j + 1)
                nc.tensor.transpose(psM[:, P:2 * P], rstd[:, j:j + 1].to_broadcast([P, P]),
                                    ident[:, :]).then_inc(rstd_mm, 1)

            def transpose_gates(c):
                pe.wait_ge(parts_ready, c + 1)
                pe.wait_ge(rstd_read, (c + 1) * TC)
                for j in range(TC):
                    last = nc.tensor.transpose(psM[0:GR, j * P:(j + 1) * P],
                                               gate_parts[:, c * TC + j, :].bitcast(F32), ident[:, :])
                last.then_inc(gT_mm, 1)

            def up(i, a, bank, done):
                c, e = divmod(i, E)
                for n, (w, v) in enumerate(((w1_hi, xn_hi), (w1_hi, xn_lo), (w1_lo, xn_hi))):
                    last = nc.tensor.matmul(bank[:, 0:CW], w[:, e, a, :], v[:, chunk(c)], start=(n == 0), stop=(n == 2))
                last.then_inc(done, 1)

            def down(i):
                c, e = divmod(i, E)
                if e == 0:
                    if c:
                        pe.wait_ge(yT_ready, c)
                    nc.tensor.matmul(psY[:, 0:CW], b2_rows[:, :], gT[:, chunk(c)], start=True, stop=False)
                pe.wait_ge(lo_done, i + 1)
                if c == 0 and e % EG == 0:
                    pe.wait_ge(w2_ready, e // EG + 1)
                for n, (w, v) in enumerate(((w2_hi, act_hi), (w2_hi, act_lo), (w2_lo, act_hi))):
                    last = nc.tensor.matmul(psY[:, 0:CW], w[:, e, :], v[:, i % 4, :], start=False,
                                            stop=(e == E - 1 and n == 2))
                last.then_inc(y_mm, 1)

            def transpose_y(c):
                pe.wait_ge(yT_ready, c + 1)
                if c:
                    pe.wait_ge(y_ready, c)
                for j in range(TC):
                    last = nc.tensor.transpose(psM[:, j * P:(j + 1) * P], yT[:, c, j * P:(j + 1) * P], ident[:, :])
                last.then_inc(y_t, 1)

            pe.wait_ge(consts_ready, 1)
            pe.wait_ge(rows_loaded, 48)
            nc.tensor.transpose(psM[:, 0:N + 2], rows[:, :], ident[0:N + 2, 0:N + 2]).then_inc(rows_t, 1)
            pe.wait_ge(x_loaded[0], 16 * TL)
            transpose_x(0, 1, psB[0])
            transpose_x(1, TC - 1, psB[1])
            pe.wait_ge(rnn_w_loaded, 32)
            pre(0)
            pe.wait_ge(rows_read, 1)
            for t in range(SC):
                step(t)
                if t < TL - 1:
                    pre(t + 1)
                if t == TL - 1:
                    pe.wait_ge(x_loaded[1], 16 * TL)
                    transpose_x(TC, TC, psG)
                if t == TL:
                    pe.wait_ge(b1_loaded, 16)
                    for a in range(2):
                        last = nc.tensor.transpose(psM[:, 64 + a * E:64 + (a + 1) * E], b1_sb[:, a::2],
                                                   ident[0:E, 0:E])
                    last.then_inc(b1_t, 1)
                if t >= TL and t % TL == 1:
                    stats(t // TL - 1)
                if t >= TL and t % TL == 3:
                    lay_rstd(t // TL - 1)
                if TL + 1 <= t < TL + 1 + TC:
                    pre(TC + t - TL - 1)
            stats(TC - 1)
            lay_rstd(TC - 1)
            for i in range(NI + LAG):
                if i < NI:
                    c, e = divmod(i, E)
                    if c == 0 and e % EG == 0:
                        pe.wait_ge(w1_ready, e // EG + 1)
                    if e == 0:
                        pe.wait_ge(xn_ready, (c + 1) * TC)
                    if i >= 2:
                        pe.wait_ge(relu_done, i - 1)
                    up(i, 0, psA[i % 2], a_mm)
                    if SC + STEPS_PER_IT * i < T:
                        step(SC + STEPS_PER_IT * i)
                    if i >= 2:
                        pe.wait_ge(lin_done, i - 1)
                    up(i, 1, psB[i % 2], b_mm)
                    if SC + STEPS_PER_IT * i + 1 < T:
                        step(SC + STEPS_PER_IT * i + 1)
                if i == 0:
                    transpose_gates(0)
                if 1 <= i <= NI:
                    c, e = divmod(i - 1, E)
                    if i == 1:
                        pe.wait_ge(select_ready, 1)
                        pe.wait_ge(b2_ready, 1)
                    if e == 0:
                        pe.wait_ge(gT_ready, c + 1)
                    if i >= 2:
                        pe.wait_ge(actg_done, i - 1)
                    nc.tensor.matmul(psG[:, 0:CW], select[:, e, :], gT[:, chunk(c)], start=True,
                                     stop=True).then_inc(g_mm, 1)
                if i >= LAG:
                    down(i - LAG)
                for j in LATE:
                    if i == square_it(j):
                        stats(j)
                    if i == square_it(j) + 1:
                        lay_rstd(j)
                if i == GATE_IT + 1:
                    transpose_gates(1)
                if i == OUT_IT - 1:
                    transpose_y(0)
            transpose_y(1)


_INS = ["x", "cond_1024", "L0_cond_Wx", "L0_cond_Wh", "L0_cond_b", "L0_ffn_norm_scale", "L0_ffn_wg", "L0_ffn_bg",
        "L0_ffn_w1", "L0_ffn_b1", "L0_ffn_w2", "L0_ffn_b2"]


def kernel(**inputs):
    import numpy as _np
    import concourse.bacc as _bacc
    from concourse import mybir as _mybir
    from concourse.bass_utils import run_bass_kernel_spmd as _run

    nc = _bacc.Bacc("TRN2", target_bir_lowering=False, num_devices=1)
    arrays, args = {}, []
    for name in _INS:
        a = _np.ascontiguousarray(inputs[name])
        arrays[f"in_{name}"] = a
        args.append(nc.dram_tensor(f"in_{name}", a.shape, _mybir.dt.from_np(a.dtype), kind="ExternalInput").ap())
    out = nc.dram_tensor("out", inputs["x"].shape, _mybir.dt.float32, kind="ExternalOutput").ap()
    adaln_rnn_moe_kernel(nc, *args, out)
    r = _run(nc, [arrays], core_ids=[0])
    return r.results[0]["out"]
```

```python
import concourse.bass as bass
from concourse import mybir
from contextlib import ExitStack



def adaln_rnn_moe_kernel(nc, x, cond, wx, wh, b, norm_scale, wg, bg, w1, b1, w2, b2, out):
    F32 = mybir.dt.float32
    F32R = mybir.dt.float32r
    U32 = mybir.dt.uint32
    ALU = mybir.AluOpType
    ACT = mybir.ActivationFunctionType
    AX = mybir.AxisListType

    N, T, D = x.shape
    E, H, I2 = w1.shape
    P = 128
    W = 512
    K = 4
    LIMIT, EPS = 7.0, 1e-05
    TL = P // N
    NT = N * T // P
    NG = 4
    EG = E // NG
    HI, LO, HI2 = 0, 32, 64
    GR = HI2 + E

    CHUNKS = [2, 2, 4]
    NC = len(CHUNKS)
    TILE0 = [sum(CHUNKS[:c]) for c in range(NC + 1)]
    EXPERTS = [W // (n * P) for n in CHUNKS]
    UNIT0 = [sum(E // r for r in EXPERTS[:c]) for c in range(NC + 1)]
    NU = UNIT0[NC]
    WARM, WARM_START, WARM_STEP = 512, 9, 2
    W1_AT = 0
    GROUP0 = list(range(CHUNKS[0])) + TILE0[1:]
    NGR = len(GROUP0) - 1
    LAG = 3
    SUM_DEPTH = 5

    STEP_SLOTS = 2
    HEAD = TL * CHUNKS[0]
    STATS = [None] + [(TL * TILE0[c + 1] - 1 - HEAD) // STEP_SLOTS + 1 for c in range(1, NC)]
    RSTD = [None] + [v + 1 for v in STATS[1:]]
    GATES = [None] + [v + 2 for v in STATS[1:]]
    GATES_T = [None] + [v + 3 for v in STATS[1:]]
    ROWS_OUT = [UNIT0[c + 1] + LAG + 2 for c in range(NC - 1)] + [None]

    ctx = ExitStack()
    with ctx:
        def sb(name, shape, dt=F32):
            return ctx.enter_context(nc.sbuf_tensor(name, shape, dt))

        def pb(name):
            return ctx.enter_context(nc.psum_tensor(name, [P, W], F32))

        def sem(name):
            return ctx.enter_context(nc.semaphore(name))

        rows = sb("rows", [N + 2, D])
        wx_sb = sb("wx_sb", [D, H])
        wh_sb = sb("wh_sb", [H, H])
        x_sb = sb("x_sb", [P, NT, D])
        b1_sb = sb("b1_sb", [E, I2])
        wg_sb = sb("wg_sb", [H, E])
        bg_sb = sb("bg_sb", [P, E])
        b2_sb = sb("b2_sb", [HI2 + E, H])
        w1_sb = sb("w1_sb", [H, E, I2])
        w2_sb = sb("w2_sb", [P, E, H])
        warm = sb("warm", [P, WARM], mybir.dt.bfloat16)
        ident = sb("ident", [P, P])
        zeros = sb("zeros", [P, P])
        ones = sb("ones", [P, 1])
        neg_half = sb("neg_half", [P, 1])
        euler = sb("euler", [P, NT * K])
        limit_col = sb("limit_col", [P, 1])
        iota_e = sb("iota_e", [P, E])
        pair_id = sb("pair_id", [P, E])
        select = sb("select", [P, E, P], F32R)
        wg_scaled = sb("wg_scaled", [H, E])
        b_col = sb("b_col", [P, 2])
        lim_b1a = sb("lim_b1a", [P, E])
        one_b1b = sb("one_b1b", [P, E])
        b2_hi = sb("b2_hi", [HI2 + E, H], F32R)
        b2_rows = sb("b2_rows", [P, H], F32R)
        w1_hi = sb("w1_hi", [H, E, 2, P], F32R)
        w1_lo = sb("w1_lo", [H, E, 2, P], F32R)
        w2_hi = sb("w2_hi", [P, E, H], F32R)
        w2_lo = sb("w2_lo", [P, E, H], F32R)
        xT = sb("xT", [D, NT * P])
        hT = sb("hT", [H, (T + 1) * N])
        xh = sb("xh", [H, NT * P])
        sq = sb("sq", [H, NT * P])
        xn = sb("xn", [H, NT * P])
        xn_hi = sb("xn_hi", [H, NT * P], F32R)
        xn_lo = sb("xn_lo", [H, NT * P], F32R)
        meansq = sb("meansq", [P, NT])
        rstd = sb("rstd", [P, NT])
        raw = sb("raw", [P, NT, E])
        logits = sb("logits", [P, NT, E])
        top = sb("top", [P, NT, 8])
        top_i = sb("top_i", [P, NT, 8], U32)
        top_f = sb("top_f", [P, NT, K])
        diff = sb("diff", [P, NT, K])
        expo = sb("expo", [P, NT, K])
        den = sb("den", [P, NT])
        inv = sb("inv", [P, NT])
        gate_k = sb("gate_k", [P, NT, K])
        hot = sb("hot", [P, NT, E, K])
        gates = sb("gates", [P, NT, E])
        gate_parts = sb("gate_parts", [P, NT, GR], F32R)
        gT = sb("gT", [P, NT * P], F32R)
        relu_a = sb("relu_a", [P, 2, W])
        swish = sb("swish", [P, 3, W])
        lin = sb("lin", [P, 2, W])
        act = sb("act", [P, 2, W])
        actg = sb("actg", [P, 3, W])
        act_hi = sb("act_hi", [P, SUM_DEPTH, W], F32R)
        act_lo = sb("act_lo", [P, SUM_DEPTH, W], F32R)
        yT = sb("yT", [P, NT * P])
        y_sb = sb("y_sb", [P, NT, D])

        psA = [pb("psA0"), pb("psA1")]
        psB = [pb("psB0"), pb("psB1")]
        psG, psY, psR, psM = pb("psG"), pb("psY"), pb("psR"), pb("psM")

        rows_loaded = sem("rows_loaded")
        x0_loaded = sem("x0_loaded")
        x_loaded = sem("x_loaded")
        wx_loaded = sem("wx_loaded")
        wh_loaded = sem("wh_loaded")
        b1_loaded = sem("b1_loaded")
        wg_loaded = sem("wg_loaded")
        bg_loaded = sem("bg_loaded")
        b2_loaded = sem("b2_loaded")
        w1_loaded = [sem(f"w1_loaded{g}") for g in range(NG)]
        w2_loaded = [sem(f"w2_loaded{g}") for g in range(NG)]
        warm_ready = sem("warm_ready")
        ident_ready = sem("ident_ready")
        consts_ready = sem("consts_ready")
        cond_ready = sem("cond_ready")
        x_t = sem("x_t")
        xT_ready = sem("xT_ready")
        wg_ready = sem("wg_ready")
        b2_rows_ready = sem("b2_rows_ready")
        select_ready = sem("select_ready")
        w1_ready = sem("w1_ready")
        w1_hi_ready = sem("w1_hi_ready")
        w2_ready = sem("w2_ready")
        m_mm = sem("m_mm")
        m_read = sem("m_read")
        step_mm = sem("step_mm")
        step_done = sem("step_done")
        sq_ready = sem("sq_ready")
        xh_ready = sem("xh_ready")
        rstd_ready = sem("rstd_ready")
        xn_ready = sem("xn_ready")
        diff_ready = sem("diff_ready")
        expo_ready = sem("expo_ready")
        parts_ready = sem("parts_ready")
        gT_ready = sem("gT_ready")
        a_mm = sem("a_mm")
        b_mm = sem("b_mm")
        g_mm = sem("g_mm")
        y_mm = sem("y_mm")
        relu_done = sem("relu_done")
        swish_done = sem("swish_done")
        lin_done = sem("lin_done")
        act_done = sem("act_done")
        actg_done = sem("actg_done")
        hi_done = sem("hi_done")
        lo_done = sem("lo_done")
        yT_ready = sem("yT_ready")
        stored = sem("stored")
        dve_chain = sem("dve_chain")
        pool_chain = sem("pool_chain")

        block = ctx.enter_context(nc.Block())

        x_v = x.rearrange("n (j s) d -> s n j d", s=TL)
        out_v = out.rearrange("n (j s) d -> s n j d", s=TL)
        w1_v = w1.rearrange("e h i -> h e i")
        w2_v = w2.rearrange("e i h -> i e h")

        def cols(c):
            return slice(TILE0[c] * P, TILE0[c + 1] * P)

        def hcols(c):
            return slice(N + TILE0[c] * P, N + TILE0[c + 1] * P)

        def tiles(c):
            return slice(TILE0[c], TILE0[c + 1])

        def group_tiles(g):
            return range(GROUP0[g], GROUP0[g + 1])

        def group_cols(g, at=0):
            return slice(at + GROUP0[g] * P, at + GROUP0[g + 1] * P)

        def last_group(c):
            return GROUP0.index(TILE0[c + 1]) - 1

        def unit(u):
            c = max(k for k in range(NC) if UNIT0[k] <= u)
            return c, (u - UNIT0[c]) * EXPERTS[c], EXPERTS[c]

        def part(c, k):
            return slice(k * CHUNKS[c] * P, (k + 1) * CHUNKS[c] * P)

        def width(u):
            c, e0, r = unit(u)
            return r * CHUNKS[c] * P

        def steps_at(u, slot):
            t = HEAD + STEP_SLOTS * u + slot
            return [t] if slot < STEP_SLOTS and t < T else []

        def step_psum(t):
            return psR[:, (t % TL) * N:(t % TL + 1) * N]

        def chunk_at(table, v):
            return [c for c in range(NC) if table[c] is not None and table[c] == v]

        def psM_turn(what):
            order = ["rows", "b1"] + [(k, g) for g in range(last_group(0) + 1) for k in ("stats", "rstd")]
            order.append(("gates", 0))
            later = []
            for c in range(1, NC):
                g = last_group(c)
                later += [(STATS[c], 1, ("stats", g)), (RSTD[c], 2, ("rstd", g)), (GATES_T[c], 3, ("gates", c))]
            later += [(ROWS_OUT[c], 4, ("out", c)) for c in range(NC - 1)]
            order += [k[2] for k in sorted(later, key=lambda k: k[:2])] + [("out", NC - 1)]
            return order.index(what) + 1

        @block.sync
        def _(sp):
            sp.dma_start(rows[0:N, :], cond).then_inc(rows_loaded, 16)
            for s in range(TL):
                sp.dma_start(x_sb[s * N:(s + 1) * N, 0:1, :], x_v[s][:, 0:1, :]).then_inc(x0_loaded, 16)
            sp.dma_start(rows[N:N + 1, :], b.rearrange("(a n) -> a n", a=1)).then_inc(rows_loaded, 16)
            sp.dma_start(rows[N + 1:N + 2, :], norm_scale.rearrange("(a n) -> a n", a=1)).then_inc(rows_loaded, 16)
            for s in range(TL):
                sp.dma_start(x_sb[s * N:(s + 1) * N, 1:NT, :], x_v[s][:, 1:NT, :]).then_inc(x_loaded, 16)
            for g in range(NG):
                ge = slice(g * EG, (g + 1) * EG)
                sp.dma_start(w1_sb[:, ge, :], w1_v[:, ge, :]).then_inc(w1_loaded[g], 16)
                sp.dma_start(w2_sb[:, ge, :], w2_v[:, ge, :]).then_inc(w2_loaded[g], 16)
            for c in range(NC):
                sp.wait_ge(m_read, psM_turn(("out", c)))
                for s in range(TL):
                    sp.dma_start(out_v[s][:, tiles(c), :], y_sb[s * N:(s + 1) * N, tiles(c), :]).then_inc(stored, 16)
            sp.wait_ge(stored, 16 * TL * NC)

        @block.gpsimd
        def _(pool):
            chain = [0]

            def link(ins):
                chain[0] += 1
                ins.then_inc(pool_chain, 1)
                pool.wait_ge(pool_chain, chain[0])

            pool.dma_start(wx_sb[:, :], wx).then_inc(wx_loaded, 16)
            pool.dma_start(wh_sb[:, :], wh).then_inc(wh_loaded, 16)
            link(nc.gpsimd.memset(zeros[:, :], 0.0))
            nc.gpsimd.affine_select(out=ident[:, :], in_=zeros[:, :], compare_op=ALU.not_equal, fill=1.0, base=0,
                                    pattern=[[-1, P]], channel_multiplier=1).then_inc(ident_ready, 1)
            pool.dma_start(wg_sb[:, :], wg).then_inc(wg_loaded, 16)
            nc.gpsimd.memset(ones[:, :], 1.0)
            nc.gpsimd.memset(neg_half[:, :], -0.5)
            nc.gpsimd.memset(euler[:, :], 2.718281828459045)
            nc.gpsimd.memset(limit_col[:, :], LIMIT)
            nc.gpsimd.iota(iota_e[:, :], pattern=[[1, E]], base=0, channel_multiplier=0,
                           allow_small_or_imprecise_dtypes=True).then_inc(consts_ready, 1)
            pool.dma_start(b1_sb[:, :], b1).then_inc(b1_loaded, 16)
            for r in (HI, LO, HI2):
                pool.dma_start(b2_sb[r:r + E, :], b2).then_inc(b2_loaded, 16)
            pool.dma_start(bg_sb[:, :], bg.partition_broadcast(P)).then_inc(bg_loaded, 16)

            def power_rstd(g):
                ts = group_tiles(g)
                pool.wait_ge(m_read, psM_turn(("stats", g)))
                nc.gpsimd.tensor_tensor(rstd[:, ts.start:ts.stop], meansq[:, ts.start:ts.stop],
                                        neg_half[:, :].to_broadcast([P, len(ts)]), ALU.pow).then_inc(rstd_ready, 1)

            def power_expo(c):
                pool.wait_ge(diff_ready, c + 1)
                nc.gpsimd.tensor_tensor(expo[:, tiles(c), :].rearrange("p j k -> p (j k)"),
                                        euler[:, 0:K * CHUNKS[c]], diff[:, tiles(c), :].rearrange("p j k -> p (j k)"),
                                        ALU.pow).then_inc(expo_ready, 1)

            def split_w2(g):
                ge = slice(g * EG, (g + 1) * EG)
                pool.wait_ge(w2_loaded[g], 16)
                link(nc.gpsimd.tensor_copy(w2_hi[:, ge, :], w2_sb[:, ge, :]))
                nc.gpsimd.tensor_tensor(w2_lo[:, ge, :], w2_sb[:, ge, :], w2_hi[:, ge, :].bitcast(F32),
                                        ALU.subtract).then_inc(w2_ready, 1)

            def add_residuals(c):
                pool.wait_ge(step_done, TL * TILE0[c + 1])
                pool.wait_ge(xT_ready, 3)
                nc.gpsimd.tensor_tensor(xh[:, cols(c)], xT[:, cols(c)], hT[:, hcols(c)], ALU.add).then_inc(xh_ready, 1)

            split_w2(0)
            power_rstd(0)
            split_w2(1)
            power_rstd(1)
            power_expo(0)
            split_w2(2)
            for v in range(NU + 1):
                if 1 <= v <= NU:
                    u = v - 1
                    pool.wait_ge(hi_done, u + 1)
                    if u >= SUM_DEPTH:
                        pool.wait_ge(y_mm, u - SUM_DEPTH + 1)
                    w = width(u)
                    nc.gpsimd.tensor_tensor(act_lo[:, u % SUM_DEPTH, 0:w], actg[:, u % 3, 0:w],
                                            act_hi[:, u % SUM_DEPTH, 0:w].bitcast(F32),
                                            ALU.subtract).then_inc(lo_done, 1)
                if v == 0:
                    split_w2(3)
                for c in chunk_at(STATS, v):
                    power_rstd(last_group(c))
                for c in chunk_at(RSTD, v):
                    power_expo(c)
                    if c == 1:
                        add_residuals(0)
                    add_residuals(c)

        @block.scalar
        def _(acte):
            acte.wait_ge(ident_ready, 1)
            nc.scalar.activation(act[:, 0, 0:1], zeros[:, 0:1], ACT.Gelu_apprx_sigmoid)

            def tanh(t):
                acte.wait_ge(step_mm, t + 1)
                nc.scalar.activation(hT[:, (t + 1) * N:(t + 2) * N], step_psum(t), ACT.Tanh,
                                     bias=b_col[:, 0:1]).then_inc(step_done, 1)

            def w1_high(g, a):
                ge = slice(g * EG, (g + 1) * EG)
                acte.wait_ge(w1_loaded[g], 16)
                nc.scalar.activation(w1_hi[:, ge, a, :], w1_sb[:, ge, a::2], ACT.Copy).then_inc(w1_hi_ready, 1)

            def act_high(u):
                acte.wait_ge(actg_done, u + 1)
                if u >= SUM_DEPTH:
                    acte.wait_ge(y_mm, u - SUM_DEPTH + 1)
                w = width(u)
                nc.scalar.activation(act_hi[:, u % SUM_DEPTH, 0:w], actg[:, u % 3, 0:w], ACT.Copy).then_inc(hi_done, 1)

            acte.wait_ge(cond_ready, 1)
            for t in range(HEAD):
                tanh(t)
                if W1_AT <= t:
                    w1_high((t - W1_AT) // 2, (t - W1_AT) % 2)
            acte.wait_ge(consts_ready, 1)
            for k in range(HEAD - W1_AT, 2 * NG):
                w1_high(k // 2, k % 2)
            for u in range(NU):
                c, e0, r = unit(u)
                if u == 0:
                    acte.wait_ge(m_read, psM_turn("b1"))
                acte.wait_ge(a_mm, u + 1)
                if u >= 2:
                    acte.wait_ge(swish_done, u - 1)
                for k in range(r):
                    o = part(c, k)
                    last = nc.scalar.activation(relu_a[:, u % 2, o], psA[u % 2][:, o], ACT.Relu, scale=-1.0,
                                                bias=lim_b1a[:, e0 + k:e0 + k + 1])
                last.then_inc(relu_done, 1)
                for t in steps_at(u, 0):
                    tanh(t)
                acte.wait_ge(relu_done, u + 1)
                if u >= 3:
                    acte.wait_ge(act_done, u - 2)
                w = width(u)
                nc.scalar.activation(swish[:, u % 3, 0:w], relu_a[:, u % 2, 0:w], ACT.Gelu_apprx_sigmoid, scale=-1.0,
                                     bias=limit_col[:, :]).then_inc(swish_done, 1)
                for t in steps_at(u, 1):
                    tanh(t)
                if u >= 1:
                    act_high(u - 1)
                for t in steps_at(u, 2):
                    tanh(t)
            act_high(NU - 1)

        @block.vector
        def _(dve):
            chain = [0]

            def link(ins):
                chain[0] += 1
                ins.then_inc(dve_chain, 1)
                dve.wait_ge(dve_chain, chain[0])

            def square(g):
                dve.wait_ge(step_done, TL * GROUP0[g + 1])
                h = hT[:, group_cols(g, N)]
                nc.vector.tensor_tensor(sq[:, group_cols(g)], h, h, ALU.mult).then_inc(sq_ready, 1)

            def stats(g):
                ts = group_tiles(g)
                n = len(ts)
                dve.wait_ge(m_mm, psM_turn(("stats", g)))
                nc.vector.tensor_copy(raw[:, ts.start:ts.stop, :],
                                      psM[:, 16:16 + n * E].rearrange("p (j e) -> p j e", e=E))
                nc.vector.tensor_scalar(meansq[:, ts.start:ts.stop], psM[:, 0:n], 1.0 / H, EPS, ALU.mult,
                                        ALU.add).then_inc(m_read, 1)

            def normalise(g):
                m = psM_turn(("rstd", g))
                dve.wait_ge(m_mm, m)
                nc.vector.scalar_tensor_tensor(xn[:, group_cols(g)], hT[:, group_cols(g, N)], b_col[:, 1:2],
                                               psM[:, 0:len(group_tiles(g)) * P], ALU.mult, ALU.mult).then_inc(m_read, 1)
                dve.wait_ge(m_read, m)
                link(nc.vector.tensor_copy(xn_hi[:, group_cols(g)], xn[:, group_cols(g)]))
                nc.vector.tensor_tensor(xn_lo[:, group_cols(g)], xn[:, group_cols(g)],
                                        xn_hi[:, group_cols(g)].bitcast(F32), ALU.subtract).then_inc(xn_ready, 1)

            def route(c):
                ts = range(TILE0[c], TILE0[c + 1])
                dve.wait_ge(rstd_ready, last_group(c) + 1)
                for j in ts:
                    last = nc.vector.scalar_tensor_tensor(logits[:, j, :], raw[:, j, :], rstd[:, j:j + 1], bg_sb[:, :],
                                                          ALU.mult, ALU.add)
                link(last)
                for j in ts:
                    last = nc.vector.max(top[:, j, :], logits[:, j, :])
                link(last)
                nc.vector.tensor_tensor(diff[:, tiles(c), :], top[:, tiles(c), 0:K],
                                        top[:, tiles(c), 0:1].to_broadcast([P, CHUNKS[c], K]),
                                        ALU.subtract).then_inc(diff_ready, 1)
                for j in ts:
                    last = nc.vector.max_index(top_i[:, j, :], top[:, j, :], logits[:, j, :])
                link(last)
                link(nc.vector.tensor_copy(top_f[:, tiles(c), :], top_i[:, tiles(c), 0:K]))
                for j in ts:
                    last = nc.vector.tensor_tensor(
                        hot[:, j, :, :], iota_e[:, :].rearrange("p (e o) -> p e o", o=1).to_broadcast([P, E, K]),
                        top_f[:, j:j + 1, :].to_broadcast([P, E, K]), ALU.is_equal)
                link(last)

            def make_gates(c):
                cj = tiles(c)
                dve.wait_ge(expo_ready, c + 1)
                link(nc.vector.tensor_reduce(den[:, cj], expo[:, cj, :], AX.X, ALU.add))
                link(nc.vector.reciprocal(inv[:, cj], den[:, cj]))
                link(nc.vector.tensor_tensor(
                    gate_k[:, cj, :], expo[:, cj, :],
                    inv[:, cj].rearrange("p (j o) -> p j o", o=1).to_broadcast([P, CHUNKS[c], K]), ALU.mult))
                for j in range(TILE0[c], TILE0[c + 1]):
                    last = nc.vector.tensor_tensor(hot[:, j, :, :], hot[:, j, :, :],
                                                   gate_k[:, j:j + 1, :].to_broadcast([P, E, K]), ALU.mult)
                link(last)
                link(nc.vector.tensor_reduce(gates[:, cj, :], hot[:, cj, :, :], AX.X, ALU.add))
                link(nc.vector.tensor_copy(gate_parts[:, cj, HI:HI + E], gates[:, cj, :]))
                nc.vector.tensor_copy(gate_parts[:, cj, HI2:HI2 + E], gates[:, cj, :])
                nc.vector.tensor_tensor(gate_parts[:, cj, LO:LO + E], gates[:, cj, :],
                                        gate_parts[:, cj, HI:HI + E].bitcast(F32),
                                        ALU.subtract).then_inc(parts_ready, 1)

            def copy_gates(c):
                m = psM_turn(("gates", c))
                dve.wait_ge(m_mm, m)
                nc.vector.tensor_copy(gT[0:GR, cols(c)], psM[0:GR, 0:CHUNKS[c] * P]).then_inc(m_read, 1)

            def w1_low(g):
                ge = slice(g * EG, (g + 1) * EG)
                for a in range(2):
                    dve.wait_ge(w1_hi_ready, 2 * g + a + 1)
                    last = nc.vector.tensor_tensor(w1_lo[:, ge, a, :], w1_sb[:, ge, a::2],
                                                   w1_hi[:, ge, a, :].bitcast(F32), ALU.subtract)
                last.then_inc(w1_ready, 1)

            def add_h(c):
                dve.wait_ge(y_mm, UNIT0[c + 1])
                dve.wait_ge(xh_ready, c + 1)
                nc.vector.tensor_tensor(yT[:, cols(c)], xh[:, cols(c)], psY[:, 0:CHUNKS[c] * P],
                                        ALU.add).then_inc(yT_ready, 1)

            def copy_rows(c):
                m = psM_turn(("out", c))
                dve.wait_ge(m_mm, m)
                nc.vector.tensor_copy(y_sb[:, tiles(c), :], psM[:, 0:CHUNKS[c] * P]
                                      .rearrange("p (j d) -> p j d", d=D)).then_inc(m_read, 1)

            nc.vector.memset(warm[:, :], 0.0).then_inc(warm_ready, 1)
            nc.vector.memset(b2_rows[:, :].bitcast(F32), 0.0)
            nc.vector.memset(gate_parts[:, :, :].bitcast(F32), 0.0)
            link(nc.vector.memset(gT[:, :].bitcast(F32), 0.0))
            dve.wait_ge(ident_ready, 1)
            link(nc.vector.tensor_tensor(pair_id[:, :], ident[:, HI:HI + E], ident[:, LO:LO + E], ALU.add))
            nc.vector.tensor_copy(select[:, :, :], pair_id[:, :].rearrange("p (e o) -> p e o", o=1)
                                  .to_broadcast([P, E, P])).then_inc(select_ready, 1)
            dve.wait_ge(m_mm, psM_turn("rows"))
            nc.vector.tensor_copy(hT[:, 0:N], psM[:, 0:N])
            nc.vector.tensor_copy(b_col[:, :], psM[:, N:N + 2]).then_inc(m_read, 1)
            dve.wait_ge(m_read, psM_turn("rows"))
            dve.wait_ge(wg_loaded, 16)
            nc.vector.tensor_scalar(wg_scaled[:, :], wg_sb[:, :], b_col[:, 1:2], None, ALU.mult).then_inc(cond_ready, 1)
            dve.wait_ge(x_t, 1)
            nc.vector.tensor_copy(xT[:, 0:P], psB[0][:, 0:P]).then_inc(xT_ready, 1)
            dve.wait_ge(x_t, 2)
            nc.vector.tensor_copy(xT[:, P:4 * P], psB[1][:, 0:3 * P]).then_inc(xT_ready, 1)
            dve.wait_ge(x_t, 3)
            nc.vector.tensor_copy(xT[:, 4 * P:NT * P], psG[:, 0:(NT - 4) * P]).then_inc(xT_ready, 1)
            dve.wait_ge(m_mm, psM_turn("b1"))
            nc.vector.tensor_scalar(lim_b1a[:, :], psM[:, 0:E], -1.0, LIMIT, ALU.mult, ALU.add)
            nc.vector.tensor_scalar(one_b1b[:, :], psM[:, E:2 * E], 1.0, None, ALU.add).then_inc(m_read, 1)
            w1_low(0)
            square(0)
            stats(0)
            normalise(0)
            dve.wait_ge(b2_loaded, 48)
            for r in (HI, LO, HI2):
                last = nc.vector.tensor_copy(b2_hi[r:r + E, :], b2_sb[r:r + E, :])
            link(last)
            nc.vector.tensor_copy(b2_rows[HI:HI + E, :], b2_sb[HI:HI + E, :])
            nc.vector.tensor_copy(b2_rows[LO:LO + E, :], b2_sb[LO:LO + E, :])
            nc.vector.tensor_tensor(b2_rows[HI2:HI2 + E, :], b2_sb[HI2:HI2 + E, :],
                                    b2_hi[HI2:HI2 + E, :].bitcast(F32), ALU.subtract).then_inc(b2_rows_ready, 1)
            w1_low(1)
            square(1)
            stats(1)
            normalise(1)
            dve.wait_ge(consts_ready, 1)
            dve.wait_ge(bg_loaded, 16)
            route(0)
            w1_low(2)
            make_gates(0)
            copy_gates(0)
            w1_low(3)

            for v in range(NU + 1):
                for c in range(NC - 1):
                    if v == UNIT0[c + 1] + LAG:
                        add_h(c)
                for c in chunk_at(GATES_T, v - 1):
                    copy_gates(c)
                for c in chunk_at(ROWS_OUT, v - 1):
                    copy_rows(c)
                if v < NU:
                    c, e0, r = unit(v)
                    dve.wait_ge(b_mm, v + 1)
                    for k in range(r):
                        o = part(c, k)
                        last = nc.vector.tensor_scalar(lin[:, v % 2, o], psB[v % 2][:, o],
                                                       one_b1b[:, e0 + k:e0 + k + 1], LIMIT + 1.0, ALU.add, ALU.min)
                    last.then_inc(lin_done, 1)
                if 1 <= v <= NU:
                    u = v - 1
                    dve.wait_ge(g_mm, u + 1)
                    dve.wait_ge(act_done, u + 1)
                    if u >= 3:
                        dve.wait_ge(lo_done, u - 2)
                    w = width(u)
                    nc.vector.tensor_tensor(actg[:, u % 3, 0:w], act[:, u % 2, 0:w], psG[:, 0:w],
                                            ALU.mult).then_inc(actg_done, 1)
                if v < NU:
                    dve.wait_ge(lin_done, v + 1)
                    dve.wait_ge(swish_done, v + 1)
                    w = width(v)
                    nc.vector.scalar_tensor_tensor(act[:, v % 2, 0:w], lin[:, v % 2, 0:w], 1.0 - LIMIT,
                                                   swish[:, v % 3, 0:w], ALU.max, ALU.mult).then_inc(act_done, 1)
                for c in chunk_at(STATS, v + 1):
                    square(last_group(c))
                for c in chunk_at(STATS, v):
                    stats(last_group(c))
                for c in chunk_at(RSTD, v):
                    route(c)
                    normalise(last_group(c))
                for c in chunk_at(GATES, v):
                    make_gates(c)
            add_h(NC - 1)
            copy_rows(NC - 1)

        @block.tensor
        def _(pe):
            def turn(what):
                if psM_turn(what) > 1:
                    pe.wait_ge(m_read, psM_turn(what) - 1)

            def transpose_x(j0, n, bank):
                for j in range(j0, j0 + n):
                    last = nc.tensor.transpose(bank[:, (j - j0) * P:(j - j0 + 1) * P], x_sb[:, j, :], ident[:, :])
                last.then_inc(x_t, 1)

            def step(t):
                if t:
                    pe.wait_ge(step_done, t)
                if t % TL == 0:
                    j = t // TL
                    pe.wait_ge(xT_ready, 1 if j == 0 else 2 if j < 4 else 3)
                    nc.tensor.matmul(psR[:, 0:P], wx_sb[:, :], xT[:, j * P:(j + 1) * P], start=True, stop=True,
                                     skip_group_check=True)
                nc.tensor.matmul(step_psum(t), wh_sb[:, :], hT[:, t * N:(t + 1) * N], start=False, stop=True,
                                 skip_group_check=True).then_inc(step_mm, 1)

            def stats(g):
                ts = group_tiles(g)
                pe.wait_ge(sq_ready, g + 1)
                turn(("stats", g))
                for k, j in enumerate(ts):
                    nc.tensor.matmul(psM[:, k:k + 1], sq[:, j * P:(j + 1) * P], ones[:, :], start=True, stop=True)
                for k, j in enumerate(ts):
                    last = nc.tensor.matmul(psM[:, 16 + k * E:16 + (k + 1) * E], hT[:, N + j * P:N + (j + 1) * P],
                                            wg_scaled[:, :], start=True, stop=True)
                last.then_inc(m_mm, 1)

            def lay_rstd(g):
                pe.wait_ge(rstd_ready, g + 1)
                turn(("rstd", g))
                for k, j in enumerate(group_tiles(g)):
                    last = nc.tensor.transpose(psM[:, k * P:(k + 1) * P], rstd[:, j:j + 1].to_broadcast([P, P]),
                                               ident[:, :])
                last.then_inc(m_mm, 1)

            def keep_warm(n):
                for _ in range(n):
                    nc.tensor.matmul(psA[1][:, 0:WARM], warm[:, 0:P], warm[:, 0:WARM], start=True, stop=True)

            def transpose_gates(c):
                pe.wait_ge(parts_ready, c + 1)
                turn(("gates", c))
                for k in range(CHUNKS[c]):
                    last = nc.tensor.transpose(psM[0:GR, k * P:(k + 1) * P],
                                               gate_parts[:, TILE0[c] + k, :].bitcast(F32), ident[:, :])
                last.then_inc(m_mm, 1)

            def up(u, a, bank, done):
                c, e0, r = unit(u)
                for k in range(r):
                    o = bank[:, part(c, k)]
                    for m, (w, x_part) in enumerate(((w1_hi, xn_hi), (w1_lo, xn_hi), (w1_hi, xn_lo))):
                        last = nc.tensor.matmul(o, w[:, e0 + k, a, :], x_part[:, cols(c)], start=(m == 0), stop=(m == 2))
                last.then_inc(done, 1)

            def lay_gates(u):
                c, e0, r = unit(u)
                n = CHUNKS[c] * P
                if u == UNIT0[c]:
                    pe.wait_ge(m_read, psM_turn(("gates", c)))
                if u >= 1:
                    pe.wait_ge(actg_done, u)
                for k in range(r):
                    last = nc.tensor.matmul(psG[:, k * n:(k + 1) * n], select[:, e0 + k, :], gT[:, cols(c)],
                                            start=True, stop=True)
                last.then_inc(g_mm, 1)

            def down(u):
                c, e0, r = unit(u)
                n = CHUNKS[c] * P
                if u == UNIT0[c]:
                    if c:
                        pe.wait_ge(yT_ready, c)
                    nc.tensor.matmul(psY[:, 0:n], b2_rows[:, :], gT[:, cols(c)], start=True, stop=False)
                pe.wait_ge(lo_done, u + 1)
                if c == 0:
                    pe.wait_ge(w2_ready, e0 // EG + 1)
                for k in range(r):
                    for m, (w, act_part) in enumerate(((w2_hi, act_hi), (w2_lo, act_hi), (w2_hi, act_lo))):
                        last = nc.tensor.matmul(psY[:, 0:n], w[:, e0 + k, :], act_part[:, u % SUM_DEPTH, part(c, k)],
                                                start=False, stop=(e0 + k == E - 1 and m == 2))
                last.then_inc(y_mm, 1)

            def transpose_out(c):
                pe.wait_ge(yT_ready, c + 1)
                turn(("out", c))
                for k in range(CHUNKS[c]):
                    j = TILE0[c] + k
                    last = nc.tensor.transpose(psM[:, k * P:(k + 1) * P], yT[:, j * P:(j + 1) * P], ident[:, :])
                last.then_inc(m_mm, 1)

            pe.wait_ge(warm_ready, 1)
            keep_warm(WARM_START)
            pe.wait_ge(ident_ready, 1)
            pe.wait_ge(rows_loaded, 48)
            nc.tensor.transpose(psM[:, 0:N + 2], rows[:, :], ident[0:N + 2, 0:N + 2]).then_inc(m_mm, 1)
            pe.wait_ge(x0_loaded, 16 * TL)
            transpose_x(0, 1, psB[0])
            pe.wait_ge(wx_loaded, 16)
            pe.wait_ge(wh_loaded, 16)
            pe.wait_ge(cond_ready, 1)
            for t in range(HEAD):
                step(t)
                if t == 0:
                    pe.wait_ge(b1_loaded, 16)
                    turn("b1")
                    for a in range(2):
                        last = nc.tensor.transpose(psM[:, a * E:(a + 1) * E], b1_sb[:, a::2], ident[0:E, 0:E])
                    last.then_inc(m_mm, 1)
                elif t == 1:
                    pe.wait_ge(x_loaded, 16 * TL)
                    transpose_x(1, 3, psB[1])
                elif t == 2:
                    transpose_x(4, NT - 4, psG)
                elif t == TL + 1:
                    pe.wait_ge(consts_ready, 1)
                    stats(0)
                elif t < HEAD - 1:
                    keep_warm(WARM_STEP)
                if t == HEAD - 1:
                    lay_rstd(0)
            stats(1)
            keep_warm(WARM_STEP)
            lay_rstd(1)
            keep_warm(WARM_STEP)
            pe.wait_ge(select_ready, 1)
            for v in range(NU + LAG):
                if v < NU:
                    c, e0, r = unit(v)
                    if c == 0:
                        pe.wait_ge(w1_ready, e0 // EG + 1)
                    if v == UNIT0[c]:
                        pe.wait_ge(xn_ready, last_group(c) + 1)
                    if v >= 2:
                        pe.wait_ge(relu_done, v - 1)
                    up(v, 0, psA[v % 2], a_mm)
                    for t in steps_at(v, 0):
                        step(t)
                    if v >= 2:
                        pe.wait_ge(lin_done, v - 1)
                    up(v, 1, psB[v % 2], b_mm)
                    for t in steps_at(v, 1):
                        step(t)
                if v == 0:
                    transpose_gates(0)
                    pe.wait_ge(b2_rows_ready, 1)
                for c in chunk_at(STATS, v):
                    stats(last_group(c))
                if 1 <= v <= NU:
                    lay_gates(v - 1)
                if v >= LAG:
                    down(v - LAG)
                for t in steps_at(v, 2):
                    step(t)
                for c in chunk_at(RSTD, v):
                    lay_rstd(last_group(c))
                for c in chunk_at(GATES_T, v):
                    transpose_gates(c)
                for c in chunk_at(ROWS_OUT, v):
                    transpose_out(c)
            transpose_out(NC - 1)


_INS = ["x", "cond_1024", "L0_cond_Wx", "L0_cond_Wh", "L0_cond_b", "L0_ffn_norm_scale", "L0_ffn_wg", "L0_ffn_bg",
        "L0_ffn_w1", "L0_ffn_b1", "L0_ffn_w2", "L0_ffn_b2"]


def kernel(**inputs):
    import numpy as _np
    import concourse.bacc as _bacc
    from concourse import mybir as _mybir
    from concourse.bass_utils import run_bass_kernel_spmd as _run

    nc = _bacc.Bacc("TRN2", target_bir_lowering=False, num_devices=1)
    arrays, args = {}, []
    for name in _INS:
        a = _np.ascontiguousarray(inputs[name])
        arrays[f"in_{name}"] = a
        args.append(nc.dram_tensor(f"in_{name}", a.shape, _mybir.dt.from_np(a.dtype), kind="ExternalInput").ap())
    out = nc.dram_tensor("out", inputs["x"].shape, _mybir.dt.float32, kind="ExternalOutput").ap()
    adaln_rnn_moe_kernel(nc, *args, out)
    r = _run(nc, [arrays], core_ids=[0])
    return r.results[0]["out"]
```

```python
import concourse.bass as bass
from concourse import mybir
from contextlib import ExitStack



def adaln_rnn_moe_kernel(nc, x, cond, wx, wh, b, norm_scale, wg, bg, w1, b1, w2, b2, out):
    F32 = mybir.dt.float32
    F32R = mybir.dt.float32r
    U32 = mybir.dt.uint32
    ALU = mybir.AluOpType
    ACT = mybir.ActivationFunctionType
    AX = mybir.AxisListType

    N, T, D = x.shape
    E, H, I2 = w1.shape
    P = 128
    W = 512
    K = 4
    LIMIT, EPS = 7.0, 1e-05
    TL = P // N
    NT = N * T // P
    NG = 4
    EG = E // NG
    NP = E // 2
    HI, LO, HI2 = 0, 32, 64

    CHUNKS = [2, 2, 4]
    NC = len(CHUNKS)
    TILE0 = [sum(CHUNKS[:c]) for c in range(NC + 1)]
    EXPERTS = [W // (n * P) for n in CHUNKS]
    UNIT0 = [sum(E // r for r in EXPERTS[:c]) for c in range(NC + 1)]
    NU = UNIT0[NC]
    WARM, WARM_START = 128, 9
    LAG = 3
    SUM_DEPTH = 5

    GROUP0 = list(range(CHUNKS[0])) + list(range(CHUNKS[0], NT + 1, 2))
    X_SPLIT = 5
    W1_SHARED = 4
    XW_TILES = W // P
    NQ = NT // 2
    PW = 2 * P

    STEP_SLOTS = 2
    W1_AT = 2
    HEAD = TL * CHUNKS[0]
    STATS = [None] + [(TL * 2 * (q + 1) - 1 - HEAD) // STEP_SLOTS + 1 for q in range(1, NQ)]
    RSTD, GATES, GATES_T = [[None] + [v + k for v in STATS[1:]] for k in (1, 3, 4)]
    ROWS_OUT = [UNIT0[c + 1] + LAG + 3 for c in range(NC - 1)] + [None]

    ctx = ExitStack()
    with ctx:
        def sb(name, shape, dt=F32):
            return ctx.enter_context(nc.sbuf_tensor(name, shape, dt))

        def pb(name):
            return ctx.enter_context(nc.psum_tensor(name, [P, W], F32))

        def sem(name):
            return ctx.enter_context(nc.semaphore(name))

        rows = sb("rows", [N + 2, D])
        wx_sb = sb("wx_sb", [D, H])
        wh_sb = sb("wh_sb", [H, H])
        x_sb = sb("x_sb", [N, T, D])
        b1_sb = sb("b1_sb", [E, I2])
        wg_sb = sb("wg_sb", [H, E])
        bg_sb = sb("bg_sb", [P, E])
        b2_sb = sb("b2_sb", [HI2 + E, H])
        w1_sb = sb("w1_sb", [H, E, I2])
        w2_sb = sb("w2_sb", [P, E, H])
        warm = sb("warm", [P, WARM], mybir.dt.bfloat16)
        ident = sb("ident", [P, P])
        zeros = sb("zeros", [P, P])
        ones = sb("ones", [P, 1])
        neg_half = sb("neg_half", [P, 1])
        euler = sb("euler", [P, 2, K - 1])
        limit_col = sb("limit_col", [P, 1])
        iota_e = sb("iota_e", [P, E])
        pair_id = sb("pair_id", [P, E])
        select = sb("select", [P, E, P], F32R)
        wg_scaled = sb("wg_scaled", [H, E])
        b_col = sb("b_col", [P, 2])
        lim_b1a = sb("lim_b1a", [P, E])
        one_b1b = sb("one_b1b", [P, E])
        b2_hi = sb("b2_hi", [HI2 + E, H], F32R)
        b2_rows = sb("b2_rows", [P, H], F32R)
        w1_hi = sb("w1_hi", [H, E, 2, P], F32R)
        w1_lo = sb("w1_lo", [H, E, 2, P], F32R)
        w2_hi = sb("w2_hi", [P, E, H], F32R)
        w2_lo = sb("w2_lo", [P, E, H], F32R)
        xT = sb("xT", [D, NT * P])
        hT = sb("hT", [H, (T + 1) * N])
        xh = sb("xh", [H, NT * P])
        sq = sb("sq", [H, NT * P])
        xn = sb("xn", [H, NT * P])
        xn_hi = sb("xn_hi", [H, NT * P], F32R)
        xn_lo = sb("xn_lo", [H, NT * P], F32R)
        meansq = sb("meansq", [P, NT])
        rstd = sb("rstd", [P, NT])
        raw = sb("raw", [P, NT, E])
        logits = sb("logits", [P, NT, E])
        top = sb("top", [P, NT, 8])
        top_i = sb("top_i", [P, NT, 8], U32)
        top_f = sb("top_f", [P, NT, K])
        diff = sb("diff", [P, NT, K])
        expo = sb("expo", [P, NT, K])
        den = sb("den", [P, NT])
        inv = sb("inv", [P, NT])
        hot = sb("hot", [P, NT, E, K])
        gate_sum = sb("gate_sum", [P, NT, E])
        gates = sb("gates", [P, NT, E])
        gate_parts = sb("gate_parts", [P, NT, P], F32R)
        gT = sb("gT", [P, NT * P], F32R)
        relu_a = sb("relu_a", [P, 2, W])
        swish = sb("swish", [P, 3, W])
        lin = sb("lin", [P, 2, W])
        act = sb("act", [P, 2, W])
        actg = sb("actg", [P, 3, W])
        act_hi = sb("act_hi", [P, SUM_DEPTH, W], F32R)
        act_lo = sb("act_lo", [P, SUM_DEPTH, W], F32R)
        yT = sb("yT", [P, NT * P])
        y_sb = sb("y_sb", [P, NT, D])

        psA = [pb("psA0"), pb("psA1")]
        psB = [pb("psB0"), pb("psB1")]
        psG, psY, psR, psM = pb("psG"), pb("psY"), pb("psR"), pb("psM")

        rows_loaded = sem("rows_loaded")
        x0_loaded = sem("x0_loaded")
        x_loaded = sem("x_loaded")
        wx_loaded = sem("wx_loaded")
        wh_loaded = sem("wh_loaded")
        b1_loaded = sem("b1_loaded")
        wg_loaded = sem("wg_loaded")
        bg_loaded = sem("bg_loaded")
        b2_loaded = sem("b2_loaded")
        w1_loaded = [sem(f"w1_loaded{g}") for g in range(NG)]
        w2_loaded = [sem(f"w2_loaded{g}") for g in range(NG)]
        warm_ready = sem("warm_ready")
        ident_ready = sem("ident_ready")
        consts_ready = sem("consts_ready")
        x_t = sem("x_t")
        xT_ready = sem("xT_ready")
        wg_ready = sem("wg_ready")
        b2_rows_ready = sem("b2_rows_ready")
        select_ready = sem("select_ready")
        w1_ready = sem("w1_ready")
        w1_half_ready = sem("w1_half_ready")
        w1_hi_ready = sem("w1_hi_ready")
        w2_hi_ready = sem("w2_hi_ready")
        w2_ready = sem("w2_ready")
        m_mm = sem("m_mm")
        raw_mm = sem("raw_mm")
        raw_read = sem("raw_read")
        m_read = sem("m_read")
        step_mm = sem("step_mm")
        step_done = sem("step_done")
        sq_ready = sem("sq_ready")
        xh_ready = sem("xh_ready")
        rstd_ready = sem("rstd_ready")
        xn_hi_ready = sem("xn_hi_ready")
        xn_ready = sem("xn_ready")
        top_ready = sem("top_ready")
        index_ready = sem("index_ready")
        hot_ready = sem("hot_ready")
        parts_ready = sem("parts_ready")
        a_mm = sem("a_mm")
        b_mm = sem("b_mm")
        g_mm = sem("g_mm")
        y_mm = sem("y_mm")
        relu_done = sem("relu_done")
        swish_done = sem("swish_done")
        lin_done = sem("lin_done")
        act_done = sem("act_done")
        actg_done = sem("actg_done")
        hi_done = sem("hi_done")
        lo_done = sem("lo_done")
        last_lo_done = sem("last_lo_done")
        yT_ready = sem("yT_ready")
        out_mm = sem("out_mm")
        rows_ready = sem("rows_ready")
        stored = sem("stored")
        dve_chain = sem("dve_chain")
        pool_chain = sem("pool_chain")

        block = ctx.enter_context(nc.Block())

        out_v = out.rearrange("n (j s) d -> s n j d", s=TL)
        w1_v = w1.rearrange("e h i -> h e i")
        w2_v = w2.rearrange("e i h -> i e h")

        def cols(c):
            return slice(TILE0[c] * P, TILE0[c + 1] * P)

        def tiles(c):
            return slice(TILE0[c], TILE0[c + 1])

        def group_tiles(g):
            return range(GROUP0[g], GROUP0[g + 1])

        def group_cols(g, at=0):
            return slice(at + GROUP0[g] * P, at + GROUP0[g + 1] * P)

        def last_group(c):
            return GROUP0.index(TILE0[c + 1]) - 1

        def pair_tiles(q):
            return range(2 * q, 2 * q + 2)

        def pair_group(q):
            return GROUP0.index(2 * q + 2) - 1

        def first_pair(c):
            return TILE0[c] // 2

        def unit(u):
            c = max(k for k in range(NC) if UNIT0[k] <= u)
            return c, (u - UNIT0[c]) * EXPERTS[c], EXPERTS[c]

        def part(c, k):
            return slice(k * CHUNKS[c] * P, (k + 1) * CHUNKS[c] * P)

        def width(u):
            c, e0, r = unit(u)
            return r * CHUNKS[c] * P

        def pieces(u):
            h = W // 2
            return [slice(0, h), slice(h, W)] if u == NU - 1 else [slice(0, width(u))]

        def gate_bank(u):
            return psM if u == NU - 1 else psG

        def steps_at(u, slot):
            t = HEAD + STEP_SLOTS * u + slot
            return [t] if slot < STEP_SLOTS and t < T else []

        def step_psum(t):
            if t < TL:
                return psY[:, t * N:(t + 1) * N]
            k = t % (TL * XW_TILES)
            return psR[:, k * N:(k + 1) * N]

        def at(table, v):
            return [k for k, w in enumerate(table) if w is not None and w == v]

        def psM_turn(what):
            order = ["rows", "b1"] + [(k, g) for g in range(last_group(0) + 1) for k in ("stats", "rstd")]
            order.append(("gates", 0))
            later = []
            for q in range(1, NQ):
                g = pair_group(q)
                later += [(STATS[q], 1, ("stats", g)), (RSTD[q], 2, ("rstd", g)), (GATES_T[q], 3, ("gates", q))]
            later += [(ROWS_OUT[c], 4, ("out", c)) for c in range(NC - 1)]
            order += [k[2] for k in sorted(later, key=lambda k: k[:2])]
            return order.index(what) + 1

        @block.sync
        def _(sp):
            sp.dma_start(rows[0:N, :], cond).then_inc(rows_loaded, 16)
            sp.dma_start(x_sb[:, 0:TL, :], x[:, 0:TL, :]).then_inc(x0_loaded, 16)
            sp.dma_start(wx_sb[:, :], wx).then_inc(wx_loaded, 16)
            sp.dma_start(rows[N:N + 1, :], b.rearrange("(a n) -> a n", a=1)).then_inc(rows_loaded, 16)
            sp.dma_start(rows[N + 1:N + 2, :], norm_scale.rearrange("(a n) -> a n", a=1)).then_inc(rows_loaded, 16)
            sp.dma_start(x_sb[:, TL:T, :], x[:, TL:T, :]).then_inc(x_loaded, 16)
            sp.dma_start(wg_sb[:, :], wg).then_inc(wg_loaded, 16)
            for g in range(NG):
                ge = slice(g * EG, (g + 1) * EG)
                sp.dma_start(w1_sb[:, ge, :], w1_v[:, ge, :]).then_inc(w1_loaded[g], 16)
                if g == 0:
                    sp.dma_start(b1_sb[:, :], b1).then_inc(b1_loaded, 16)
                if g == 1:
                    sp.dma_start(bg_sb[:, :], bg.partition_broadcast(P)).then_inc(bg_loaded, 16)
                sp.dma_start(w2_sb[:, ge, :], w2_v[:, ge, :]).then_inc(w2_loaded[g], 16)
            for r in (HI, LO, HI2):
                sp.dma_start(b2_sb[r:r + E, :], b2).then_inc(b2_loaded, 16)
            for c in range(NC):
                if c < NC - 1:
                    sp.wait_ge(m_read, psM_turn(("out", c)))
                else:
                    sp.wait_ge(rows_ready, 2)
                for s in range(TL):
                    sp.dma_start(out_v[s][:, tiles(c), :], y_sb[s * N:(s + 1) * N, tiles(c), :]).then_inc(stored, 16)
            sp.wait_ge(stored, 16 * TL * NC)

        @block.gpsimd
        def _(pool):
            chain = [0]

            def link(ins):
                chain[0] += 1
                ins.then_inc(pool_chain, 1)
                pool.wait_ge(pool_chain, chain[0])

            pool.dma_start(wh_sb[:, :], wh).then_inc(wh_loaded, 16)
            link(nc.gpsimd.memset(zeros[:, :], 0.0))
            nc.gpsimd.affine_select(out=ident[:, :], in_=zeros[:, :], compare_op=ALU.not_equal, fill=1.0, base=0,
                                    pattern=[[-1, P]], channel_multiplier=1).then_inc(ident_ready, 1)
            nc.gpsimd.memset(ones[:, :], 1.0)
            nc.gpsimd.memset(neg_half[:, :], -0.5)
            nc.gpsimd.memset(euler[:, :, :], 2.718281828459045)
            nc.gpsimd.memset(limit_col[:, :], LIMIT)
            nc.gpsimd.memset(expo[:, :, 0:1], 1.0)
            nc.gpsimd.iota(iota_e[:, :], pattern=[[1, E]], base=0, channel_multiplier=0,
                           allow_small_or_imprecise_dtypes=True)
            nc.gpsimd.memset(gate_parts[:, :, :].bitcast(F32), 0.0).then_inc(consts_ready, 1)
            pool.wait_ge(consts_ready, 1)

            def power_rstd(g):
                ts = group_tiles(g)
                pool.wait_ge(m_read, psM_turn(("stats", g)))
                nc.gpsimd.tensor_tensor(rstd[:, ts.start:ts.stop], meansq[:, ts.start:ts.stop],
                                        neg_half[:, :].to_broadcast([P, len(ts)]), ALU.pow).then_inc(rstd_ready, 1)

            def power_expo(q):
                tq = slice(2 * q, 2 * q + 2)
                pool.wait_ge(top_ready, q + 1)
                chain[0] += 1
                nc.gpsimd.tensor_tensor(expo[:, tq, 1:K], euler[:, :, :], diff[:, tq, 1:K],
                                        ALU.pow).then_inc(pool_chain, 1)

            def place_expo(q):
                pool.wait_ge(pool_chain, chain[0])
                pool.wait_ge(index_ready, q + 1)
                for j in pair_tiles(q):
                    last = nc.gpsimd.tensor_tensor(hot[:, j, :, :], hot[:, j, :, :],
                                                   expo[:, j:j + 1, :].to_broadcast([P, E, K]), ALU.mult)
                last.then_inc(hot_ready, 1)

            def xn_low(g):
                pool.wait_ge(xn_hi_ready, g - CHUNKS[0] + 1)
                nc.gpsimd.tensor_tensor(xn_lo[:, group_cols(g)], xn[:, group_cols(g)],
                                        xn_hi[:, group_cols(g)].bitcast(F32), ALU.subtract).then_inc(xn_ready, 1)

            def w2_low(p):
                pool.wait_ge(w2_hi_ready, p + 1)
                pe_ = slice(2 * p, 2 * p + 2)
                nc.gpsimd.tensor_tensor(w2_lo[:, pe_, :], w2_sb[:, pe_, :], w2_hi[:, pe_, :].bitcast(F32),
                                        ALU.subtract).then_inc(w2_ready, 1)

            def w1_low(p):
                pool.wait_ge(w1_hi_ready, 2 * p + 2)
                pe_ = slice(2 * p, 2 * p + 2)
                nc.gpsimd.tensor_tensor(w1_lo[:, pe_, 1, :], w1_sb[:, pe_, 1::2], w1_hi[:, pe_, 1, :].bitcast(F32),
                                        ALU.subtract).then_inc(w1_half_ready, 1)

            def add_residuals(q):
                qc = slice(q * PW, (q + 1) * PW)
                pool.wait_ge(step_done, 2 * TL * (q + 1))
                pool.wait_ge(xT_ready, 3)
                nc.gpsimd.tensor_tensor(xh[:, qc], xT[:, qc], hT[:, N + q * PW:N + (q + 1) * PW],
                                        ALU.add).then_inc(xh_ready, 1)

            power_rstd(0)
            power_rstd(1)
            w2_low(0)
            power_expo(0)
            place_expo(0)
            w2_low(1)
            w2_low(2)
            for v in range(NU + 1):
                for q in at(RSTD, v - 1):
                    xn_low(pair_group(q))
                    place_expo(q)
                if 1 <= v <= NU - 1:
                    u = v - 1
                    pool.wait_ge(hi_done, u + 1)
                    if u >= SUM_DEPTH:
                        pool.wait_ge(y_mm, u - SUM_DEPTH + 1)
                    w = width(u)
                    nc.gpsimd.tensor_tensor(act_lo[:, u % SUM_DEPTH, 0:w], actg[:, u % 3, 0:w],
                                            act_hi[:, u % SUM_DEPTH, 0:w].bitcast(F32),
                                            ALU.subtract).then_inc(lo_done, 1)
                for q in at(STATS, v):
                    power_rstd(pair_group(q))
                if W1_SHARED <= v + 3 < NP:
                    w1_low(v + 3)
                if v + 3 < NP:
                    w2_low(v + 3)
                for q in at(RSTD, v):
                    power_expo(q)
                for q in at(GATES, v):
                    if q == 1:
                        add_residuals(0)
                    add_residuals(q)

        @block.scalar
        def _(acte):
            acte.wait_ge(ident_ready, 1)
            nc.scalar.activation(act[:, 0, 0:1], zeros[:, 0:1], ACT.Gelu_apprx_sigmoid)

            def tanh(t):
                acte.wait_ge(step_mm, t + 1)
                nc.scalar.activation(hT[:, (t + 1) * N:(t + 2) * N], step_psum(t), ACT.Tanh,
                                     bias=b_col[:, 0:1]).then_inc(step_done, 1)

            def w1_high(k):
                p, a = k // 2, k % 2
                pe_ = slice(2 * p, 2 * p + 2)
                acte.wait_ge(w1_loaded[2 * p // EG], 16)
                nc.scalar.activation(w1_hi[:, pe_, a, :], w1_sb[:, pe_, a::2], ACT.Copy).then_inc(w1_hi_ready, 1)

            def w2_high(p):
                pe_ = slice(2 * p, 2 * p + 2)
                acte.wait_ge(w2_loaded[2 * p // EG], 16)
                nc.scalar.activation(w2_hi[:, pe_, :], w2_sb[:, pe_, :], ACT.Copy).then_inc(w2_hi_ready, 1)

            def square(g):
                acte.wait_ge(step_done, TL * GROUP0[g + 1])
                nc.scalar.activation(sq[:, group_cols(g)], hT[:, group_cols(g, N)], ACT.Square).then_inc(sq_ready, 1)

            def copy_gates(q):
                m = psM_turn(("gates", q))
                acte.wait_ge(m_mm, m)
                nc.scalar.activation(gT[:, q * PW:(q + 1) * PW], psM[:, 0:PW], ACT.Copy).then_inc(m_read, 1)

            def copy_rows(c):
                m = psM_turn(("out", c))
                acte.wait_ge(m_mm, m)
                nc.scalar.activation(y_sb[:, tiles(c), :].rearrange("p j d -> p (j d)"), psM[:, 0:CHUNKS[c] * P],
                                     ACT.Copy).then_inc(m_read, 1)

            def act_high(u):
                if u >= SUM_DEPTH:
                    acte.wait_ge(y_mm, u - SUM_DEPTH + 1)
                for k, o in enumerate(pieces(u)):
                    acte.wait_ge(actg_done, u + 1 + k)
                    nc.scalar.activation(act_hi[:, u % SUM_DEPTH, o], actg[:, u % 3, o],
                                         ACT.Copy).then_inc(hi_done, 1)

            acte.wait_ge(m_read, psM_turn("rows"))
            for t in range(HEAD):
                tanh(t)
                if t == TL:
                    square(0)
                elif t == HEAD - 1:
                    square(1)
                elif W1_AT <= t:
                    w1_high(t - W1_AT - (t > TL))
            acte.wait_ge(consts_ready, 1)
            for k in range(HEAD - W1_AT - 2, 2 * NP):
                w1_high(k)
                if k >= 2 * NP - 3:
                    w2_high(k - 2 * NP + 3)
            for u in range(NU):
                for q in at(GATES_T, u - 1):
                    copy_gates(q)
                for c in at(ROWS_OUT, u - 1):
                    copy_rows(c)
                c, e0, r = unit(u)
                if u == 0:
                    acte.wait_ge(m_read, psM_turn("b1"))
                acte.wait_ge(a_mm, u + 1)
                if u >= 2:
                    acte.wait_ge(swish_done, u - 1)
                for k in range(r):
                    if k == 1:
                        for t in steps_at(u, 0):
                            tanh(t)
                    o = part(c, k)
                    last = nc.scalar.activation(relu_a[:, u % 2, o], psA[u % 2][:, o], ACT.Relu, scale=-1.0,
                                                bias=lim_b1a[:, e0 + k:e0 + k + 1])
                last.then_inc(relu_done, 1)
                acte.wait_ge(relu_done, u + 1)
                if u >= 3:
                    acte.wait_ge(act_done, u - 2)
                w = width(u)
                nc.scalar.activation(swish[:, u % 3, 0:w], relu_a[:, u % 2, 0:w], ACT.Gelu_apprx_sigmoid, scale=-1.0,
                                     bias=limit_col[:, :]).then_inc(swish_done, 1)
                for t in steps_at(u, 1):
                    tanh(t)
                for q in at(STATS, u + 1):
                    square(pair_group(q))
                if u >= 1:
                    act_high(u - 1)
                if u + 3 < NP:
                    w2_high(u + 3)
            act_high(NU - 1)
            acte.wait_ge(out_mm, 1)
            nc.scalar.activation(y_sb[:, NT - 4:NT - 2, :].rearrange("p j d -> p (j d)"), psA[0][:, 0:PW],
                                 ACT.Copy).then_inc(rows_ready, 1)

        @block.vector
        def _(dve):
            chain = [0]

            def link(ins):
                chain[0] += 1
                ins.then_inc(dve_chain, 1)
                dve.wait_ge(dve_chain, chain[0])

            def stats(g):
                ts = group_tiles(g)
                n = len(ts)
                dve.wait_ge(m_mm, psM_turn(("stats", g)))
                mean = nc.vector.tensor_scalar(meansq[:, ts.start:ts.stop], psM[:, 0:n], 1.0 / H, EPS, ALU.mult,
                                               ALU.add)
                if g < CHUNKS[0]:
                    mean.then_inc(m_read, 1)
                else:
                    copy_raw(ts, psM).then_inc(m_read, 1)

            def copy_raw(ts, bank):
                return nc.vector.tensor_copy(raw[:, ts.start:ts.stop, :], bank[:, 16:16 + len(ts) * E]
                                             .rearrange("p (j e) -> p j e", e=E))

            def normalise(g):
                m = psM_turn(("rstd", g))
                dve.wait_ge(m_mm, m)
                nc.vector.scalar_tensor_tensor(xn[:, group_cols(g)], hT[:, group_cols(g, N)], b_col[:, 1:2],
                                               psM[:, 0:len(group_tiles(g)) * P], ALU.mult, ALU.mult).then_inc(m_read, 1)
                dve.wait_ge(m_read, m)
                hi = nc.vector.tensor_copy(xn_hi[:, group_cols(g)], xn[:, group_cols(g)])
                if g >= CHUNKS[0]:
                    hi.then_inc(xn_hi_ready, 1)
                    return
                link(hi)
                nc.vector.tensor_tensor(xn_lo[:, group_cols(g)], xn[:, group_cols(g)],
                                        xn_hi[:, group_cols(g)].bitcast(F32), ALU.subtract).then_inc(xn_ready, 1)

            def mark(ins):
                chain[0] += 1
                ins.then_inc(dve_chain, 1)

            def settled():
                dve.wait_ge(dve_chain, chain[0])

            def route_logits(q):
                dve.wait_ge(rstd_ready, pair_group(q) + 1)
                for j in pair_tiles(q):
                    last = nc.vector.scalar_tensor_tensor(logits[:, j, :], raw[:, j, :], rstd[:, j:j + 1], bg_sb[:, :],
                                                          ALU.mult, ALU.add)
                mark(last)

            def route_top(q):
                settled()
                for j in pair_tiles(q):
                    last = nc.vector.max(top[:, j, :], logits[:, j, :])
                mark(last)

            def route_index(q):
                settled()
                ts = slice(2 * q, 2 * q + 2)
                nc.vector.tensor_tensor(diff[:, ts, :], top[:, ts, 0:K], top[:, ts, 0:1].to_broadcast([P, 2, K]),
                                        ALU.subtract).then_inc(top_ready, 1)
                for j in pair_tiles(q):
                    last = nc.vector.max_index(top_i[:, j, :], top[:, j, :], logits[:, j, :])
                mark(last)

            def route_float(q):
                settled()
                mark(nc.vector.tensor_copy(top_f[:, 2 * q:2 * q + 2, :], top_i[:, 2 * q:2 * q + 2, 0:K]))

            def route_hot(q):
                settled()
                for j in pair_tiles(q):
                    last = nc.vector.tensor_tensor(
                        hot[:, j, :, :], iota_e[:, :].rearrange("p (e o) -> p e o", o=1).to_broadcast([P, E, K]),
                        top_f[:, j:j + 1, :].to_broadcast([P, E, K]), ALU.is_equal)
                last.then_inc(index_ready, 1)

            def gates_sum(q):
                dve.wait_ge(hot_ready, q + 1)
                ts = slice(2 * q, 2 * q + 2)
                nc.vector.tensor_reduce(gate_sum[:, ts, :], hot[:, ts, :, :], AX.X, ALU.add)
                mark(nc.vector.tensor_reduce(den[:, ts], expo[:, ts, :], AX.X, ALU.add))

            def gates_inverse(q):
                settled()
                mark(nc.vector.reciprocal(inv[:, 2 * q:2 * q + 2], den[:, 2 * q:2 * q + 2]))

            def gates_scale(q):
                settled()
                ts = slice(2 * q, 2 * q + 2)
                mark(nc.vector.tensor_tensor(
                    gates[:, ts, :], gate_sum[:, ts, :],
                    inv[:, ts].rearrange("p (j o) -> p j o", o=1).to_broadcast([P, 2, E]), ALU.mult))

            def gates_high(q):
                settled()
                ts = slice(2 * q, 2 * q + 2)
                mark(nc.vector.tensor_copy(
                    gate_parts[:, ts, :].rearrange("p j (a e) -> p j a e", a=P // HI2)[:, :, :, 0:E],
                    gates[:, ts, :].rearrange("p j (o e) -> p j o e", o=1).to_broadcast([P, 2, P // HI2, E])))

            def gates_low(q):
                settled()
                ts = slice(2 * q, 2 * q + 2)
                nc.vector.tensor_tensor(gate_parts[:, ts, LO:LO + E], gates[:, ts, :],
                                        gate_parts[:, ts, HI:HI + E].bitcast(F32),
                                        ALU.subtract).then_inc(parts_ready, 1)

            def copy_gates(q):
                m = psM_turn(("gates", q))
                dve.wait_ge(m_mm, m)
                nc.vector.tensor_copy(gT[:, q * PW:(q + 1) * PW], psM[:, 0:PW]).then_inc(m_read, 1)

            def w1_low(p):
                pe_ = slice(2 * p, 2 * p + 2)
                for a in range(2 if p < W1_SHARED else 1):
                    dve.wait_ge(w1_hi_ready, 2 * p + a + 1)
                    last = nc.vector.tensor_tensor(w1_lo[:, pe_, a, :], w1_sb[:, pe_, a::2],
                                                   w1_hi[:, pe_, a, :].bitcast(F32), ALU.subtract)
                last.then_inc(w1_ready, 1)

            def round_b2():
                dve.wait_ge(b2_loaded, 48)
                link(nc.vector.tensor_copy(b2_hi[HI2:HI2 + E, :], b2_sb[HI2:HI2 + E, :]))
                nc.vector.tensor_copy(b2_rows[HI:HI + E, :], b2_sb[HI:HI + E, :])
                nc.vector.tensor_copy(b2_rows[LO:LO + E, :], b2_sb[LO:LO + E, :])
                nc.vector.tensor_tensor(b2_rows[HI2:HI2 + E, :], b2_sb[HI2:HI2 + E, :],
                                        b2_hi[HI2:HI2 + E, :].bitcast(F32), ALU.subtract).then_inc(b2_rows_ready, 1)

            def add_h(c):
                dve.wait_ge(y_mm, UNIT0[c + 1])
                dve.wait_ge(xh_ready, first_pair(c + 1))
                nc.vector.tensor_tensor(yT[:, cols(c)], xh[:, cols(c)], psY[:, 0:CHUNKS[c] * P],
                                        ALU.add).then_inc(yT_ready, 1)

            nc.vector.memset(warm[:, :], 0.0).then_inc(warm_ready, 1)
            nc.vector.memset(b2_rows[:, :].bitcast(F32), 0.0)
            dve.wait_ge(m_mm, psM_turn("rows"))
            nc.vector.tensor_copy(hT[:, 0:N], psM[:, 0:N])
            nc.vector.tensor_copy(b_col[:, :], psM[:, N:N + 2]).then_inc(m_read, 1)
            dve.wait_ge(x_t, 1)
            nc.vector.tensor_copy(xT[:, 0:P], psB[0][:, 0:P]).then_inc(xT_ready, 1)
            dve.wait_ge(m_read, psM_turn("rows"))
            dve.wait_ge(wg_loaded, 16)
            nc.vector.tensor_scalar(wg_scaled[:, :], wg_sb[:, :], b_col[:, 1:2], None, ALU.mult).then_inc(wg_ready, 1)
            dve.wait_ge(x_t, 2)
            nc.vector.tensor_copy(xT[:, P:4 * P], psB[1][:, 0:3 * P]).then_inc(xT_ready, 1)
            dve.wait_ge(ident_ready, 1)
            link(nc.vector.tensor_tensor(pair_id[:, :], ident[:, HI:HI + E], ident[:, LO:LO + E], ALU.add))
            nc.vector.tensor_copy(select[:, :, :], pair_id[:, :].rearrange("p (e o) -> p e o", o=1)
                                  .to_broadcast([P, E, P])).then_inc(select_ready, 1)
            dve.wait_ge(m_mm, psM_turn("b1"))
            nc.vector.tensor_scalar(lim_b1a[:, :], psM[:, 0:E], -1.0, LIMIT, ALU.mult, ALU.add)
            nc.vector.tensor_scalar(one_b1b[:, :], psM[:, E:2 * E], 1.0, None, ALU.add).then_inc(m_read, 1)
            w1_low(0)
            stats(0)
            w1_low(1)
            normalise(0)
            stats(1)
            dve.wait_ge(raw_mm, 1)
            copy_raw(pair_tiles(0), psB[0]).then_inc(raw_read, 1)
            round_b2()
            dve.wait_ge(consts_ready, 1)
            dve.wait_ge(bg_loaded, 16)
            normalise(1)
            route_logits(0)
            route_top(0)
            route_index(0)
            route_float(0)
            route_hot(0)
            w1_low(2)
            dve.wait_ge(x_t, 3)
            nc.vector.tensor_copy(xT[:, 4 * P:NT * P], psG[:, 0:(NT - 4) * P]).then_inc(xT_ready, 1)
            gates_sum(0)
            gates_inverse(0)
            gates_scale(0)
            gates_high(0)
            gates_low(0)

            for v in range(NU + 1):
                for c in range(NC - 1):
                    if v == UNIT0[c + 1] + LAG:
                        add_h(c)
                for q in at(RSTD, v - 1):
                    normalise(pair_group(q))
                for q in at(GATES_T, v):
                    gates_low(q)
                if v < NU:
                    c, e0, r = unit(v)
                    dve.wait_ge(b_mm, v + 1)
                    for k in range(r):
                        o = part(c, k)
                        last = nc.vector.tensor_scalar(lin[:, v % 2, o], psB[v % 2][:, o],
                                                       one_b1b[:, e0 + k:e0 + k + 1], LIMIT + 1.0, ALU.add, ALU.min)
                    last.then_inc(lin_done, 1)
                for q in at(STATS, v):
                    stats(pair_group(q))
                for q in at(RSTD, v):
                    route_logits(q)
                for q in at(RSTD, v - 1):
                    route_float(q)
                for q in at(GATES, v):
                    gates_sum(q)
                if 1 <= v <= NU:
                    u = v - 1
                    dve.wait_ge(g_mm, u + 1)
                    dve.wait_ge(act_done, u + 1)
                    if u >= 3:
                        dve.wait_ge(lo_done, u - 2)
                    for o in pieces(u):
                        nc.vector.tensor_tensor(actg[:, u % 3, o], act[:, u % 2, o], gate_bank(u)[:, o],
                                                ALU.mult).then_inc(actg_done, 1)
                for q in at(RSTD, v):
                    route_top(q)
                for q in at(RSTD, v - 1):
                    route_hot(q)
                for q in at(GATES, v):
                    gates_inverse(q)
                if v < NU:
                    dve.wait_ge(lin_done, v + 1)
                    dve.wait_ge(swish_done, v + 1)
                    w = width(v)
                    nc.vector.scalar_tensor_tensor(act[:, v % 2, 0:w], lin[:, v % 2, 0:w], 1.0 - LIMIT,
                                                   swish[:, v % 3, 0:w], ALU.max, ALU.mult).then_inc(act_done, 1)
                if v + 3 < NP:
                    w1_low(v + 3)
                if v == 0:
                    copy_gates(0)
                for q in at(RSTD, v):
                    route_index(q)
                for q in at(GATES, v):
                    gates_scale(q)
                    gates_high(q)
                if v == NU:
                    u = v - 1
                    for k, o in enumerate(pieces(u)):
                        dve.wait_ge(hi_done, u + 1 + k)
                        nc.vector.tensor_tensor(act_lo[:, u % SUM_DEPTH, o], actg[:, u % 3, o],
                                                act_hi[:, u % SUM_DEPTH, o].bitcast(F32),
                                                ALU.subtract).then_inc(last_lo_done, 1)
            dve.wait_ge(y_mm, NU)
            dve.wait_ge(xh_ready, NQ)
            for k in range(2):
                o = slice((NT - 4 + 2 * k) * P, (NT - 2 + 2 * k) * P)
                nc.vector.tensor_tensor(yT[:, o], xh[:, o], psY[:, k * PW:(k + 1) * PW], ALU.add).then_inc(yT_ready, 1)
            dve.wait_ge(out_mm, 2)
            nc.vector.tensor_copy(y_sb[:, NT - 2:NT, :], psA[1][:, 0:PW].rearrange("p (j d) -> p j d", d=D)
                                  ).then_inc(rows_ready, 1)

        @block.tensor
        def _(pe):
            def turn(what):
                if psM_turn(what) > 1:
                    pe.wait_ge(m_read, psM_turn(what) - 1)

            def transpose_x(j, bank, k):
                for s in range(TL):
                    o = k * P + s * N
                    last = nc.tensor.transpose(bank[:, o:o + N], x_sb[:, j * TL + s, :], ident[0:N, 0:N])
                return last

            def x_wx(j, n):
                pe.wait_ge(xT_ready, 1 if j == 0 else 2 if j < XW_TILES else 3)
                k = j % XW_TILES
                bank = psY if j == 0 else psR
                nc.tensor.matmul(bank[:, k * P:(k + n) * P], wx_sb[:, :], xT[:, j * P:(j + n) * P], start=True,
                                 stop=True, skip_group_check=True)

            def step(t):
                if t:
                    pe.wait_ge(step_done, t)
                if t == XW_TILES * TL:
                    x_wx(XW_TILES, NT - XW_TILES)
                nc.tensor.matmul(step_psum(t), wh_sb[:, :], hT[:, t * N:(t + 1) * N], start=False, stop=True,
                                 skip_group_check=True).then_inc(step_mm, 1)

            def sums(g):
                pe.wait_ge(sq_ready, g + 1)
                turn(("stats", g))
                for k, j in enumerate(group_tiles(g)):
                    last = nc.tensor.matmul(psM[:, k:k + 1], sq[:, j * P:(j + 1) * P], ones[:, :], start=True, stop=True)
                return last

            def raw_logits(ts, bank):
                for k, j in enumerate(ts):
                    last = nc.tensor.matmul(bank[:, 16 + k * E:16 + (k + 1) * E], hT[:, N + j * P:N + (j + 1) * P],
                                            wg_scaled[:, :], start=True, stop=True)
                return last

            def lay_rstd(g):
                pe.wait_ge(rstd_ready, g + 1)
                turn(("rstd", g))
                for k, j in enumerate(group_tiles(g)):
                    last = nc.tensor.transpose(psM[:, k * P:(k + 1) * P], rstd[:, j:j + 1].to_broadcast([P, P]),
                                               ident[:, :])
                last.then_inc(m_mm, 1)

            def keep_warm(n):
                for _ in range(n):
                    nc.tensor.matmul(psA[1][:, 0:WARM], warm[:, 0:P], warm[:, 0:WARM], start=True, stop=True)

            def transpose_gates(q):
                pe.wait_ge(parts_ready, q + 1)
                turn(("gates", q))
                for k, j in enumerate(pair_tiles(q)):
                    last = nc.tensor.transpose(psM[:, k * P:(k + 1) * P], gate_parts[:, j, :].bitcast(F32),
                                               ident[:, :])
                last.then_inc(m_mm, 1)

            def up(u, a, bank, done):
                c, e0, r = unit(u)
                for k in range(r):
                    o = bank[:, part(c, k)]
                    for m, (w, x_part) in enumerate(((w1_hi, xn_hi), (w1_lo, xn_hi), (w1_hi, xn_lo))):
                        last = nc.tensor.matmul(o, w[:, e0 + k, a, :], x_part[:, cols(c)], start=(m == 0), stop=(m == 2))
                last.then_inc(done, 1)

            def lay_gates(u):
                c, e0, r = unit(u)
                n = CHUNKS[c] * P
                if u == UNIT0[c]:
                    pe.wait_ge(m_read, psM_turn(("gates", first_pair(c + 1) - 1)))
                if u == NU - 1:
                    pe.wait_ge(m_read, psM_turn(("out", NC - 2)))
                elif u >= 1:
                    pe.wait_ge(actg_done, u)
                for k in range(r):
                    last = nc.tensor.matmul(gate_bank(u)[:, k * n:(k + 1) * n], select[:, e0 + k, :], gT[:, cols(c)],
                                            start=True, stop=True)
                last.then_inc(g_mm, 1)

            def down(u):
                c, e0, r = unit(u)
                n = CHUNKS[c] * P
                if u == UNIT0[c]:
                    if c:
                        pe.wait_ge(yT_ready, c)
                    nc.tensor.matmul(psY[:, 0:n], b2_rows[:, :], gT[:, cols(c)], start=True, stop=False)
                pe.wait_ge(hi_done, u + len(pieces(u)))
                if c == 0:
                    pe.wait_ge(w2_ready, (e0 + r - 1) // 2 + 1)
                for k in range(r):
                    for w in (w2_hi, w2_lo):
                        nc.tensor.matmul(psY[:, 0:n], w[:, e0 + k, :], act_hi[:, u % SUM_DEPTH, part(c, k)],
                                         start=False, stop=False)
                if u < NU - 1:
                    pe.wait_ge(lo_done, u + 1)
                else:
                    pe.wait_ge(last_lo_done, len(pieces(u)))
                for k in range(r):
                    last = nc.tensor.matmul(psY[:, 0:n], w2_hi[:, e0 + k, :], act_lo[:, u % SUM_DEPTH, part(c, k)],
                                            start=False, stop=(e0 + k == E - 1))
                last.then_inc(y_mm, 1)

            def transpose_out(c):
                pe.wait_ge(yT_ready, c + 1)
                turn(("out", c))
                for k in range(CHUNKS[c]):
                    j = TILE0[c] + k
                    last = nc.tensor.transpose(psM[:, k * P:(k + 1) * P], yT[:, j * P:(j + 1) * P], ident[:, :])
                last.then_inc(m_mm, 1)

            pe.wait_ge(warm_ready, 1)
            keep_warm(WARM_START)
            pe.wait_ge(ident_ready, 1)
            pe.wait_ge(rows_loaded, 48)
            nc.tensor.transpose(psM[:, 0:N + 2], rows[:, :], ident[0:N + 2, 0:N + 2]).then_inc(m_mm, 1)
            pe.wait_ge(x0_loaded, 16)
            transpose_x(0, psB[0], 0).then_inc(x_t, 1)
            pe.wait_ge(wx_loaded, 16)
            pe.wait_ge(wh_loaded, 16)
            pe.wait_ge(m_read, psM_turn("rows"))
            x_wx(0, 1)
            for t in range(HEAD):
                step(t)
                if t == 0:
                    pe.wait_ge(x_loaded, 16)
                if t < 3:
                    last = transpose_x(t + 1, psB[1], t)
                if t == 2:
                    last.then_inc(x_t, 1)
                if t == 3:
                    x_wx(1, 1)
                if t == 4:
                    pe.wait_ge(b1_loaded, 16)
                    turn("b1")
                    for a in range(2):
                        last = nc.tensor.transpose(psM[:, a * E:(a + 1) * E], b1_sb[:, a::2], ident[0:E, 0:E])
                    last.then_inc(m_mm, 1)
                if t == TL + 1:
                    pe.wait_ge(consts_ready, 1)
                    sums(0).then_inc(m_mm, 1)
                if 3 <= t < HEAD - 1:
                    keep_warm(1)
                if t == HEAD - 1:
                    lay_rstd(0)
            sums(1).then_inc(m_mm, 1)
            pe.wait_ge(wg_ready, 1)
            raw_logits(pair_tiles(0), psB[0]).then_inc(raw_mm, 1)
            for j in range(4, NT):
                if j == X_SPLIT:
                    lay_rstd(1)
                last = transpose_x(j, psG, j - 4)
            last.then_inc(x_t, 1)
            x_wx(2, XW_TILES - 2)
            for v in range(NU + LAG):
                if v < NU:
                    c, e0, r = unit(v)
                    if c == 0:
                        pe.wait_ge(w1_ready, (e0 + r - 1) // 2 + 1)
                    if v == UNIT0[c]:
                        pe.wait_ge(xn_ready, last_group(c) + 1)
                    if v >= 2:
                        pe.wait_ge(relu_done, v - 1)
                    up(v, 0, psA[v % 2], a_mm)
                    for t in steps_at(v, 0):
                        step(t)
                    if v == 1:
                        transpose_gates(0)
                        pe.wait_ge(b2_rows_ready, 1)
                        pe.wait_ge(select_ready, 1)
                    for q in at(STATS, v):
                        sums(pair_group(q))
                        raw_logits(pair_tiles(q), psM).then_inc(m_mm, 1)
                    if v >= 2:
                        pe.wait_ge(lin_done, v - 1)
                    if v == 0:
                        pe.wait_ge(raw_read, 1)
                    if c == 0 and (e0 + r - 1) // 2 >= W1_SHARED:
                        pe.wait_ge(w1_half_ready, (e0 + r - 1) // 2 - W1_SHARED + 1)
                    up(v, 1, psB[v % 2], b_mm)
                if 1 <= v <= NU:
                    lay_gates(v - 1)
                for t in steps_at(v, 1):
                    step(t)
                if v >= LAG:
                    down(v - LAG)
                for q in at(RSTD, v):
                    lay_rstd(pair_group(q))
                for q in at(GATES_T, v):
                    transpose_gates(q)
                for c in at(ROWS_OUT, v):
                    transpose_out(c)
            for k in range(2):
                pe.wait_ge(yT_ready, NC + k)
                for i in range(2):
                    j = NT - 4 + 2 * k + i
                    last = nc.tensor.transpose(psA[k][:, i * P:(i + 1) * P], yT[:, j * P:(j + 1) * P], ident[:, :])
                last.then_inc(out_mm, 1)


_INS = ["x", "cond_1024", "L0_cond_Wx", "L0_cond_Wh", "L0_cond_b", "L0_ffn_norm_scale", "L0_ffn_wg", "L0_ffn_bg",
        "L0_ffn_w1", "L0_ffn_b1", "L0_ffn_w2", "L0_ffn_b2"]


def kernel(**inputs):
    import numpy as _np
    import concourse.bacc as _bacc
    from concourse import mybir as _mybir
    from concourse.bass_utils import run_bass_kernel_spmd as _run

    nc = _bacc.Bacc("TRN2", target_bir_lowering=False, num_devices=1)
    arrays, args = {}, []
    for name in _INS:
        a = _np.ascontiguousarray(inputs[name])
        arrays[f"in_{name}"] = a
        args.append(nc.dram_tensor(f"in_{name}", a.shape, _mybir.dt.from_np(a.dtype), kind="ExternalInput").ap())
    out = nc.dram_tensor("out", inputs["x"].shape, _mybir.dt.float32, kind="ExternalOutput").ap()
    adaln_rnn_moe_kernel(nc, *args, out)
    r = _run(nc, [arrays], core_ids=[0])
    return r.results[0]["out"]
```
